# Optimizing a Trainium2 kernel written in Bass

```python
import numpy as np
import jax
import jax.numpy as jnp

def _softmax(x, axis=-1):
    return jax.nn.softmax(x, axis=axis)

def _gelu(x):
    return jax.nn.gelu(x, approximate=True)

def _silu(x):
    return jax.nn.silu(x)

def _sigmoid(x):
    return jax.nn.sigmoid(x)

def _layernorm(x, axis=-1, eps=1e-05):
    m = jnp.mean(x, axis=axis, keepdims=True)
    v = jnp.var(x, axis=axis, keepdims=True)
    return (x - m) / jnp.sqrt(v + eps)

def _scatter_add(tgt, idx, src, axis=0):
    return tgt.at[idx].add(src)

def _segment_sum(src, seg, n):
    return jax.ops.segment_sum(src, seg, n)
kernel_name = 'mk_sandwich_d1_jaxref_r4_effb8f'

def setup_inputs(seed: int=0):
    np.random.seed(seed)
    _w = jnp.asarray

    def _L0_attn_setup():
        import jax, jax.numpy as jnp
        import numpy as np
        BW_EPS = 0.0001

        def _bump_sorted(v_sorted, z_sort, log_bw):
            B, H, L, D = v_sorted.shape
            v = v_sorted.reshape(B * H, L, D).astype(jnp.float32)
            z = z_sort.reshape(B * H, L).astype(jnp.float32)
            bw = jax.nn.softplus(log_bw.astype(jnp.float32)) + BW_EPS
            bw = jnp.broadcast_to(bw[None, :], (B, H)).reshape(B * H, 1)
            P_v = jnp.cumsum(v, axis=1)
            P_zv = jnp.cumsum(v * z[..., None], axis=1)
            zpad = jnp.zeros((B * H, 1, D), jnp.float32)
            P_v_pad = jnp.concatenate([zpad, P_v], axis=1)
            P_zv_pad = jnp.concatenate([zpad, P_zv], axis=1)
            left_idx = jax.vmap(lambda a, q: jnp.searchsorted(a, q, side='left'))(z, z - bw)
            rightp1 = jax.vmap(lambda a, q: jnp.searchsorted(a, q, side='right'))(z, z + bw)
            gather = lambda P, idx: jnp.take_along_axis(P, idx[..., None], axis=1)
            sum_v_left = P_v - gather(P_v_pad, left_idx)
            sum_zv_left = P_zv - gather(P_zv_pad, left_idx)
            sum_v_right = gather(P_v_pad, rightp1) - P_v
            sum_zv_right = gather(P_zv_pad, rightp1) - P_zv
            inv_bw = (1.0 / bw)[..., None]
            z_over = (z / bw)[..., None]
            out = sum_v_left * (1.0 - z_over) + sum_zv_left * inv_bw + sum_v_right * (1.0 + z_over) - sum_zv_right * inv_bw
            return out.reshape(B, H, L, D)

        def _forward(hidden_states, Wq, bq, Wk, bk, Wv, bv, Wproj, log_bandwidth, num_heads=16):
            B, T, Hs = hidden_states.shape
            H = num_heads
            D = Hs // H
            heads = lambda y: jnp.transpose(y.reshape(B, T, H, D), (0, 2, 1, 3))
            q = heads(hidden_states @ Wq.T + bq)
            k = heads(hidden_states @ Wk.T + bk)
            v = heads(hidden_states @ Wv.T + bv)
            q_proj = q.reshape(B, T, H * D) @ Wproj.T
            k_proj = k.reshape(B, T, H * D) @ Wproj.T
            Z = jnp.transpose(jnp.concatenate([k_proj, q_proj], axis=1), (0, 2, 1))
            Zf = Z.astype(jnp.float32)
            idx = jnp.argsort(Zf, axis=2)
            z_sort = jnp.take_along_axis(Zf, idx, axis=2)
            inv_idx = jnp.argsort(idx, axis=2)
            v_exp = jnp.concatenate([v, jnp.zeros_like(v)], axis=2)
            v_sorted = jnp.take_along_axis(v_exp, idx[..., None], axis=2)
            ctx_sorted = _bump_sorted(v_sorted, z_sort, log_bandwidth).astype(v.dtype)
            ctx = jnp.take_along_axis(ctx_sorted, inv_idx[..., None], axis=2)[:, :, T:]
            ctx = ctx / jnp.asarray(T, ctx.dtype)
            return jnp.transpose(ctx, (0, 2, 1, 3)).reshape(B, T, H * D)
        key = jax.random.key(seed)
        ks = jax.random.split(key, 6)
        B, T, Hs, H = (4, 512, 256, 16)
        s = 0.02
        return {'hidden_states': jax.random.normal(ks[0], (B, T, Hs), jnp.float32), 'Wq': jax.random.normal(ks[1], (Hs, Hs), jnp.float32) * s, 'bq': jnp.zeros((Hs,), jnp.float32), 'Wk': jax.random.normal(ks[2], (Hs, Hs), jnp.float32) * s, 'bk': jnp.zeros((Hs,), jnp.float32), 'Wv': jax.random.normal(ks[3], (Hs, Hs), jnp.float32) * s, 'bv': jnp.zeros((Hs,), jnp.float32), 'Wproj': jax.random.normal(ks[4], (H, Hs), jnp.float32) * s, 'log_bandwidth': jnp.zeros((H,), jnp.float32)}
    _L0_attn_in = _L0_attn_setup()

    def _L0_ffn_setup():
        import jax, jax.numpy as jnp
        import numpy as np
        TOP_K = 8
        CAPACITY = 128

        def _silu(x):
            return x * jax.nn.sigmoid(x)
        key = jax.random.key(seed)
        ks = jax.random.split(key, 7)
        B, S, H, E, I, Is = (2, 256, 256, 64, 128, 512)
        s = 0.05
        return {'hidden_states': jax.random.normal(ks[0], (B, S, H), jnp.float32), 'gate_w': jax.random.normal(ks[1], (H, E), jnp.float32) * s, 'shared_gate_w': jax.random.normal(ks[2], (H, 1), jnp.float32) * s, 'shared_gate_up_w': jax.random.normal(ks[3], (H, 2 * Is), jnp.float32) * s, 'shared_down_w': jax.random.normal(ks[4], (Is, H), jnp.float32) * s, 'expert_gate_up_w': jax.random.normal(ks[5], (E, H, 2 * I), jnp.float32) * s, 'expert_down_w': jax.random.normal(ks[6], (E, I, H), jnp.float32) * s}
    _L0_ffn_in = _L0_ffn_setup()
    _d = {'L0_attn_hidden_states': _L0_attn_in['hidden_states'], 'L0_attn_Wq': _L0_attn_in['Wq'], 'L0_attn_bq': _L0_attn_in['bq'], 'L0_attn_Wk': _L0_attn_in['Wk'], 'L0_attn_bk': _L0_attn_in['bk'], 'L0_attn_Wv': _L0_attn_in['Wv'], 'L0_attn_bv': _L0_attn_in['bv'], 'L0_attn_Wproj': _L0_attn_in['Wproj'], 'L0_attn_log_bandwidth': _L0_attn_in['log_bandwidth'], 'L0_ffn_gate_w': _L0_ffn_in['gate_w'], 'L0_ffn_shared_gate_w': _L0_ffn_in['shared_gate_w'], 'L0_ffn_shared_gate_up_w': _L0_ffn_in['shared_gate_up_w'], 'L0_ffn_shared_down_w': _L0_ffn_in['shared_down_w'], 'L0_ffn_expert_gate_up_w': _L0_ffn_in['expert_gate_up_w'], 'L0_ffn_expert_down_w': _L0_ffn_in['expert_down_w']}
    _x0 = _d['L0_attn_hidden_states']
    _d['L0_attn_hidden_states'] = jax.random.normal(jax.random.fold_in(jax.random.key(seed), 1), (4, 2048, 256), dtype=_x0.dtype)
    del _x0
    return _d

def reference(L0_attn_hidden_states, L0_attn_Wq, L0_attn_bq, L0_attn_Wk, L0_attn_bk, L0_attn_Wv, L0_attn_bv, L0_attn_Wproj, L0_attn_log_bandwidth, L0_ffn_gate_w, L0_ffn_shared_gate_w, L0_ffn_shared_gate_up_w, L0_ffn_shared_down_w, L0_ffn_expert_gate_up_w, L0_ffn_expert_down_w):

    def _L0_attn_ref(hidden_states, Wq, bq, Wk, bk, Wv, bv, Wproj, log_bandwidth):
        import jax, jax.numpy as jnp
        import numpy as np
        BW_EPS = 0.0001

        def _bump_sorted(v_sorted, z_sort, log_bw):
            B, H, L, D = v_sorted.shape
            v = v_sorted.reshape(B * H, L, D).astype(jnp.float32)
            z = z_sort.reshape(B * H, L).astype(jnp.float32)
            bw = jax.nn.softplus(log_bw.astype(jnp.float32)) + BW_EPS
            bw = jnp.broadcast_to(bw[None, :], (B, H)).reshape(B * H, 1)
            P_v = jnp.cumsum(v, axis=1)
            P_zv = jnp.cumsum(v * z[..., None], axis=1)
            zpad = jnp.zeros((B * H, 1, D), jnp.float32)
            P_v_pad = jnp.concatenate([zpad, P_v], axis=1)
            P_zv_pad = jnp.concatenate([zpad, P_zv], axis=1)
            left_idx = jax.vmap(lambda a, q: jnp.searchsorted(a, q, side='left'))(z, z - bw)
            rightp1 = jax.vmap(lambda a, q: jnp.searchsorted(a, q, side='right'))(z, z + bw)
            gather = lambda P, idx: jnp.take_along_axis(P, idx[..., None], axis=1)
            sum_v_left = P_v - gather(P_v_pad, left_idx)
            sum_zv_left = P_zv - gather(P_zv_pad, left_idx)
            sum_v_right = gather(P_v_pad, rightp1) - P_v
            sum_zv_right = gather(P_zv_pad, rightp1) - P_zv
            inv_bw = (1.0 / bw)[..., None]
            z_over = (z / bw)[..., None]
            out = sum_v_left * (1.0 - z_over) + sum_zv_left * inv_bw + sum_v_right * (1.0 + z_over) - sum_zv_right * inv_bw
            return out.reshape(B, H, L, D)

        def _forward(hidden_states, Wq, bq, Wk, bk, Wv, bv, Wproj, log_bandwidth, num_heads=16):
            B, T, Hs = hidden_states.shape
            H = num_heads
            D = Hs // H
            heads = lambda y: jnp.transpose(y.reshape(B, T, H, D), (0, 2, 1, 3))
            q = heads(hidden_states @ Wq.T + bq)
            k = heads(hidden_states @ Wk.T + bk)
            v = heads(hidden_states @ Wv.T + bv)
            q_proj = q.reshape(B, T, H * D) @ Wproj.T
            k_proj = k.reshape(B, T, H * D) @ Wproj.T
            Z = jnp.transpose(jnp.concatenate([k_proj, q_proj], axis=1), (0, 2, 1))
            Zf = Z.astype(jnp.float32)
            idx = jnp.argsort(Zf, axis=2)
            z_sort = jnp.take_along_axis(Zf, idx, axis=2)
            inv_idx = jnp.argsort(idx, axis=2)
            v_exp = jnp.concatenate([v, jnp.zeros_like(v)], axis=2)
            v_sorted = jnp.take_along_axis(v_exp, idx[..., None], axis=2)
            ctx_sorted = _bump_sorted(v_sorted, z_sort, log_bandwidth).astype(v.dtype)
            ctx = jnp.take_along_axis(ctx_sorted, inv_idx[..., None], axis=2)[:, :, T:]
            ctx = ctx / jnp.asarray(T, ctx.dtype)
            return jnp.transpose(ctx, (0, 2, 1, 3)).reshape(B, T, H * D)
        return _forward(hidden_states, Wq, bq, Wk, bk, Wv, bv, Wproj, log_bandwidth, num_heads=16)

    def _L0_ffn_ref(hidden_states, gate_w, shared_gate_w, shared_gate_up_w, shared_down_w, expert_gate_up_w, expert_down_w):
        import jax, jax.numpy as jnp
        import numpy as np
        TOP_K = 8
        CAPACITY = 128

        def _silu(x):
            return x * jax.nn.sigmoid(x)
        B, S, H = hidden_states.shape
        x = hidden_states.reshape(-1, H)
        T = x.shape[0]
        E = gate_w.shape[1]
        Is = shared_gate_up_w.shape[1] // 2
        I = expert_gate_up_w.shape[2] // 2
        gu = x @ shared_gate_up_w
        shared = _silu(gu[:, :Is]) * gu[:, Is:] @ shared_down_w
        shared = shared * jax.nn.sigmoid(x @ shared_gate_w)
        logits = x @ gate_w
        probs = jax.nn.softmax(logits.astype(jnp.float32), axis=-1)
        w, idx = jax.lax.top_k(probs, TOP_K)
        w = (w / jnp.sum(w, axis=-1, keepdims=True)).astype(x.dtype)
        e_flat = idx.reshape(-1)
        w_flat = w.reshape(-1)
        A = e_flat.shape[0]
        tok = jnp.arange(A) // TOP_K
        onehot = jax.nn.one_hot(e_flat, E, dtype=jnp.int32)
        pos = jnp.take_along_axis(jnp.cumsum(onehot, axis=0) - 1, e_flat[:, None], axis=1)[:, 0]
        slot = jnp.minimum(pos, CAPACITY)
        buf = jnp.zeros((E, CAPACITY + 1, H), x.dtype).at[e_flat, slot].set(x[tok])
        gu_e = jnp.einsum('ech,ehf->ecf', buf, expert_gate_up_w)
        act = _silu(gu_e[..., :I]) * gu_e[..., I:]
        out_e = jnp.einsum('eci,eih->ech', act, expert_down_w)
        y = out_e[e_flat, slot] * w_flat[:, None]
        y = jnp.where((pos < CAPACITY)[:, None], y, jnp.zeros_like(y))
        y = y.reshape(T, TOP_K, H).sum(axis=1)
        return (y + shared).reshape(B, S, H)
    x = L0_attn_hidden_states
    x = x + _layernorm(_L0_attn_ref(_layernorm(x, axis=-1), L0_attn_Wq, L0_attn_bq, L0_attn_Wk, L0_attn_bk, L0_attn_Wv, L0_attn_bv, L0_attn_Wproj, L0_attn_log_bandwidth), axis=-1)
    x = x + _layernorm(_L0_ffn_ref(_layernorm(x, axis=-1), L0_ffn_gate_w, L0_ffn_shared_gate_w, L0_ffn_shared_gate_up_w, L0_ffn_shared_down_w, L0_ffn_expert_gate_up_w, L0_ffn_expert_down_w), axis=-1)
    return x

_drawn_inputs = setup_inputs


def setup_inputs(seed=0):
    import zlib

    import numpy as np

    out = dict(_drawn_inputs(seed))
    spreads = {'L0_attn_bq': (0.0, 0.283),
     'L0_attn_bk': (0.0, 0.696),
     'L0_attn_bv': (0.0, 0.1),
     'L0_attn_log_bandwidth': (0.0, 0.467)}
    factors = {'L0_attn_Wk': 4.813}
    for name, (base, spread) in spreads.items():
        noise = np.random.default_rng([zlib.crc32(name.encode()), seed]).standard_normal(out[name].shape)
        drawn = base * np.exp(spread * noise) if base else spread * noise
        out[name] = jnp.asarray(drawn.astype(out[name].dtype))
    for name, factor in factors.items():
        out[name] = (out[name] * factor).astype(out[name].dtype)
    return out
```

```python
import concourse.bass as bass
from concourse import mybir
from contextlib import ExitStack

fp32 = mybir.dt.float32
u32 = mybir.dt.uint32
i32 = mybir.dt.int32
ALU = mybir.AluOpType
ACT = mybir.ActivationFunctionType
AX = mybir.AxisListType

NB, NT, C, H, D = 4, 2048, 256, 16, 16
KB = NT // 128
NE, CAP, TOPK = 64, 128, 8
NI, NS = 128, 512
TOK = NB * NT
NTILE = TOK // 128
NZB = 5
NTB = 6
VW = KB * C + 16


class Stream:

    def __init__(self, eng, sem):
        self.eng, self.sem, self.n, self.reached = eng, sem, 0, {}

    def wait(self, *after):
        for t in after:
            if t is not None and t[1] > self.reached.get(id(t[0]), 0):
                self.eng.wait_ge(t[0], t[1])
                self.reached[id(t[0])] = t[1]

    def op(self, fn, *after, inc=True):
        self.wait(*after)
        ins = fn(self.eng)
        if inc:
            ins.then_inc(self.sem, 1)
            self.n += 1
        return (self.sem, self.n)

    def transfer(self, line, fn, *after):
        self.wait(*after)
        fn(self.eng).then_inc(line.sem, 16)
        line.n += 16
        return (line.sem, line.n)

    def dma(self, line, out, in_, *after):
        return self.transfer(line, lambda e: e.dma_start(out, in_), *after)

    def last(self):
        return (self.sem, self.n)


class Line:

    def __init__(self, sem):
        self.sem, self.n = sem, 0

    def done(self):
        return (self.sem, self.n) if self.n else None


def view(a, offset, dims):
    return bass.AP(a.tensor, a.offset + offset, [list(a.ap[0])] + [list(d) for d in dims])


def build(nc, x, WqT, bq, WkT, bk, WvT, bv, WpT, lbw, gates_w, sgu_w, sdn_w, egu_w, edn_w, out):
    with ExitStack() as ctx:
        def sb(name, shape, dt=fp32):
            return ctx.enter_context(nc.sbuf_tensor(name, shape, dt))

        def dram(name, shape):
            return nc.dram_tensor(name, shape, fp32, kind="Internal").ap()

        def line(name):
            return Line(ctx.enter_context(nc.semaphore(name)))

        PE = Stream(nc.tensor, ctx.enter_context(nc.semaphore("s_pe")))
        AC = Stream(nc.scalar, ctx.enter_context(nc.semaphore("s_act")))
        DV = Stream(nc.vector, ctx.enter_context(nc.semaphore("s_dve")))
        PL = Stream(nc.gpsimd, ctx.enter_context(nc.semaphore("s_pool")))
        SP = Stream(nc.sync, ctx.enter_context(nc.semaphore("s_sp")))

        ZQ = dram("zq_rows", (NB, H, H, 128))
        XH = dram("h_rows", (TOK + 128, C + NE))
        X1 = dram("x1_rows", (TOK, C))
        Y = dram("y_rows", (TOK + 128, C))
        CUM = dram("cum_rows", (NE, NTILE, 128))
        BASE = dram("base_row", (1, NE * NTILE))

        TB = sb("TB", [128, NTB * NT])
        ZB = sb("ZB", [128, NZB * NT])
        V = [sb(f"V{i}", [128, VW]) for i in range(2)]
        ctxT = sb("ctxT", [128, NT])
        ctxn = sb("ctxn", [128, KB, C])
        scr = sb("scr", [128, 5120])
        BD = sb("BD", [128, 16, 128])
        wq_sb = sb("wq_sb", [128, 2, C])
        wk_sb = sb("wk_sb", [128, 2, C])
        wv_sb = sb("wv_sb", [128, 2, C])
        wg_sb = sb("wg_sb", [128, 2, NE + 1])
        wsgu = sb("wsgu", [128, 2, 2 * NS])
        wsdn = sb("wsdn", [128, 4, C])
        bqc = sb("bqc", [128, 2])
        bkc = sb("bkc", [128, 2])
        bvb = sb("bvb", [128, C])
        ident = sb("ident", [128, 128])
        bb = sb("bb", [128, H])
        bt = sb("bt", [128, 3, H])
        sB = sb("sB", [128, H])
        nzk = [sb(f"nzk{i}", [128, C]) for i in range(2)]
        mhalf = sb("mhalf", [128, 16])
        st6 = sb("st6", [128, 4, 6])
        mv = sb("mv", [128, 4, 2])
        ve = sb("ve", [128, 4])
        rs = sb("rs", [128, 4])
        Lg = sb("Lg", [128, KB, NE + 1])
        sg = sb("sg", [128, KB])
        carry = sb("carry", [NE, 1])
        bs = sb("bs", [NE, NTILE])

        scol = sb("scol", [128, 1])
        scoli = sb("scoli", [128, 1], i32)

        ps = [ctx.enter_context(nc.psum_tensor(f"ps{i}", [128, 512], fp32)) for i in range(8)]
        bank_free = [None] * 8

        xT_v = x.rearrange("b (k i p) c -> b k p i c", p=128, i=4)
        X1v = X1.rearrange("(n i p) c -> n p i c", p=128, i=4)
        XHv = XH[0:TOK, :].rearrange("(n i p) c -> n p i c", p=128, i=4)
        Yv = Y[0:TOK, :].rearrange("(n i p) c -> n p i c", p=128, i=4)
        outv = out.rearrange("b (k i p) c -> (b k) p i c", p=128, i=4)

        l_w = line("l_w")
        l_zero = line("l_zero")
        l_sgu = line("l_sgu")
        for dst, src in ((wq_sb, WqT), (wk_sb, WkT), (wv_sb, WvT)):
            SP.dma(l_w, dst[:, :, :], src.rearrange("(k p) n -> p k n", p=128))
        for dst, src in ((bqc, bq), (bkc, bk)):
            SP.dma(l_w, dst[:, :], src)
        SP.dma(l_w, bvb[:, :], bass.AP(bv.tensor, bv.offset, [[0, 128], [1, C]]))
        SP.dma(l_w, bb[:, :], bass.AP(lbw.tensor, lbw.offset, [[0, 128], [1, H]]))
        bd0 = PL.op(lambda e: e.memset(BD[:, :, :], 0.0))
        w_ready = None
        for h in range(8):
            w_ready = SP.dma(l_w, BD[16 * h:16 * h + 16, :, 16 * h:16 * h + 16], WpT, bd0)
        SP.dma(l_sgu, wg_sb[:, :, :], gates_w.rearrange("(k p) n -> p k n", p=128))
        SP.dma(l_sgu, wsgu[:, :, :], sgu_w.rearrange("(k p) n -> p k n", p=128))
        wf_ready = SP.dma(l_sgu, wsdn[:, :, :], sdn_w.rearrange("(k p) n -> p k n", p=128))

        i0 = PL.op(lambda e: e.memset(ident[:, :], 0.0))
        id_ready = PL.op(lambda e: e.affine_select(out=ident[:, :], in_=ident[:, :], compare_op=ALU.not_equal,
                                                   fill=1.0, base=0, pattern=[[-1, 128]], channel_multiplier=1), i0)
        mh_ready = PL.op(lambda e: e.memset(mhalf[:, :], -0.5))
        io = PL.op(lambda e: e.iota(scoli[:, :], pattern=[[0, 1]], base=0, channel_multiplier=1))
        s_ready = PL.op(lambda e: e.tensor_copy(scol[:, :], scoli[:, :]), io)
        DV.op(lambda e: e.memset(carry[:, :], 0.0))
        for i in range(2):
            v_pad = DV.op(lambda e, i=i: e.memset(V[i][:, KB * C:VW], 0.0))
        z = DV.op(lambda e: e.memset(scr[:, 0:C + NE], 0.0))
        z = SP.dma(l_zero, XH[TOK:TOK + 128, :], scr[:, 0:C + NE], z)
        z = SP.dma(l_zero, Y[TOK:TOK + 128, :], scr[:, 0:C])
        zero_sent = z

        t = AC.op(lambda e: e.activation(bt[:, 0, :], bb[:, :], ACT.Abs), w_ready)
        t = AC.op(lambda e: e.activation(bt[:, 1, :], bt[:, 0, :], ACT.Exp, scale=-1.0), t)
        t = AC.op(lambda e: e.activation(bt[:, 2, :], bt[:, 1, :], ACT.Ln, bias=1.0), t)
        t1 = DV.op(lambda e: e.tensor_scalar(bt[:, 0, :], bb[:, :], 0.0, None, ALU.max), t)
        t2 = DV.op(lambda e: e.tensor_tensor(bt[:, 1, :], bt[:, 0, :], bt[:, 2, :], ALU.add), t1)
        b_ready = DV.op(lambda e: e.tensor_scalar(bb[:, :], bt[:, 1, :], 1e-4, None, ALU.add), t2)
        t3 = DV.op(lambda e: e.tensor_scalar(bt[:, 0, :], bb[:, :], -float(NT), None, ALU.mult), b_ready)
        sB_ready = DV.op(lambda e: e.reciprocal(sB[:, :], bt[:, 0, :]), t3)

        def take(bank, *after):
            return [bank_free[bank], *after]

        rot = [4]

        def next_bank():
            k = rot[0]
            rot[0] = 4 + (k - 3) % 3
            return k

        ln_free = [None]

        def rstd(ap4, *after):
            for i in range(4):
                a = DV.op(lambda e, i=i: e.bn_stats(st6[:, i, :], ap4(i)), *after, ln_free[0])
            for i in range(4):
                m = DV.op(lambda e, i=i: e.bn_aggr(mv[:, i, :], st6[:, i, :]), a)
            p = PL.op(lambda e: e.tensor_scalar(ve[:, :], view(mv[:, 0, 1:2], 0, [[2, 4]]), 1e-5, None, ALU.add),
                      m, ln_free[0])
            return PL.op(lambda e: e.tensor_tensor(rs[:, :], ve[:, :], mhalf[:, 0:4], ALU.pow), p, mh_ready)

        def normalize(dst4, src4, *ready):
            for i in range(4):
                n = DV.op(lambda e, i=i: e.tensor_scalar(dst4(i), src4(i), mv[:, i, 0:1], rs[:, i:i + 1],
                                                         ALU.subtract, ALU.mult), *ready)
            ln_free[0] = n
            return n

        def transposes(dst_banks, src4, ready):
            for c in range(2):
                for i in range(4):
                    p = PE.op(lambda e, c=c, i=i: e.transpose(ps[dst_banks[c]][:, 128 * i:128 * i + 128],
                                                              src4(i)[:, 128 * c:128 * c + 128], ident[:, :]),
                              *take(dst_banks[c], ready, id_ready), inc=(i == 3))
            return p

        l_x = [line("l_x0"), line("l_x1")]
        l_zq = line("l_zq")
        front = {}
        scr_free = [zero_sent]
        V_free = [None, None]

        def front_gen(b):
            par = b % 2
            xg = [view(scr[:, 0:1], 1024 * i, [[256, 4], [1, 256]]) for i in range(2)]
            hT = view(scr[:, 0:1], 2048, [[1024, 2], [1, 1024]])
            QK = view(scr[:, 0:1], 4096, [[1, 1024]])
            Zs = view(Lg[:, 0, 0:1], 0, [[256, 2], [128, 2], [1, 128]])
            phase = list(scr_free)
            v_done = None
            hT_free = None
            qk_free = None
            xg_free = [None, None]
            for hf in range(2):
                for g in range(2):
                    blk = 2 * hf + g
                    xa = xg[g]
                    ld = SP.dma(l_x[g], xa, xT_v[b, blk], *phase, xg_free[g])
                    yield
                    yield
                    yield
                    r = rstd(lambda i: xa[:, i, :], ld)
                    yield
                    yield
                    n = normalize(lambda i: xa[:, i, :], lambda i: xa[:, i, :], r)
                    yield
                    bk2 = [next_bank(), next_bank()]
                    p = transposes(bk2, lambda i: xa[:, i, :], n)
                    xg_free[g] = p
                    yield
                    for c in range(2):
                        f = AC if c else DV
                        if c:
                            ev = AC.op(lambda e, c=c: e.activation(hT[:, c, 512 * g:512 * g + 512], ps[bk2[c]][:, :],
                                                                   ACT.Copy), p, hT_free)
                        else:
                            ev0 = DV.op(lambda e, c=c: e.tensor_copy(hT[:, c, 512 * g:512 * g + 512],
                                                                     ps[bk2[c]][:, :]), p, hT_free)
                        bank_free[bk2[c]] = ev if c else ev0
                    yield
                    for pair in range(2):
                        k = next_bank()
                        for i in range(2):
                            ti = 2 * pair + i
                            for c in range(2):
                                p = PE.op(lambda e, k=k, i=i, c=c, ti=ti: e.matmul(
                                    ps[k][:, 256 * i:256 * i + 256],
                                    hT[:, c, 512 * g + 128 * ti:512 * g + 128 * ti + 128],
                                    wv_sb[:, c, :], start=(c == 0), stop=(c == 1)),
                                    *take(k, ev, ev0, w_ready), inc=(i == 1 and c == 1))
                        o = (4 * blk + 2 * pair) * C
                        v_done = DV.op(lambda e, k=k, o=o: e.tensor_tensor(
                            view(V[par][:, o:o + 1], 0, [[256, 2], [1, 256]]),
                            view(ps[k][:, 0:1], 0, [[256, 2], [1, 256]]),
                            view(bvb[:, 0:1], 0, [[0, 2], [1, 256]]), ALU.add), p, V_free[par], v_pad)
                        bank_free[k] = v_done
                        yield
                for pj, (w, bias) in enumerate(((wq_sb, bqc), (wk_sb, bkc))):
                    for m in range(2):
                        for n2 in range(2):
                            k = next_bank()
                            for c in range(2):
                                p = PE.op(lambda e, k=k, c=c, n2=n2, m=m, w=w: e.matmul(
                                    ps[k][:, :], w[:, c, 128 * m:128 * m + 128],
                                    hT[:, c, 512 * n2:512 * n2 + 512], start=(c == 0), stop=(c == 1)),
                                    *take(k, ev, ev0, w_ready), inc=(c == 1))
                            q = AC.op(lambda e, k=k, n2=n2, m=m, bias=bias: e.activation(
                                QK[:, 512 * n2:512 * n2 + 512], ps[k][:, :], ACT.Identity,
                                bias=bias[:, m:m + 1]), p, qk_free, *phase)
                            bank_free[k] = q
                            yield
                        hT_free = p
                        k = next_bank()
                        for tt in range(16):
                            p = PE.op(lambda e, k=k, tt=tt: e.matmul(
                                ps[k][:, 0:64], BD[:, tt, :], view(QK[:, 0:1], tt, [[16, 64]]),
                                start=(tt == 0), stop=(tt == 15)), *take(k, q), inc=(tt == 15))
                            if tt % 4 == 3:
                                yield
                        qk_free = p
                        zc = DV.op(lambda e, k=k, pj=pj, m=m, hf=hf: e.tensor_copy(
                            Zs[:, pj, m, 64 * hf:64 * hf + 64], ps[k][:, 0:64]), p, *phase)
                        bank_free[k] = zc
                        yield
            zq = None
            for m in range(2):
                dst = bass.AP(ZQ.tensor, ZQ[b].offset + m * 8 * H * 128, [[128, 128], [1, 128]])
                zq = SP.dma(l_zq, dst, Zs[:, 0, m, :], zc)
            k = next_bank()
            for m in range(2):
                p = PE.op(lambda e, k=k, m=m: e.transpose(ps[k][:, 128 * m:128 * m + 128], Zs[:, 1, m, :],
                                                          ident[:, :]), *take(k, zc), inc=(m == 1))
            nz = DV.op(lambda e, k=k: e.tensor_scalar(nzk[par][:, :], ps[k][:, 0:256], -1.0, None, ALU.mult),
                       p, V_free[par])
            bank_free[k] = nz
            scr_free[:] = [PE.last(), nz, AC.last(), zq]
            front[b] = (zq, v_done, nz)
            yield

        l_a = line("l_a")
        l_h = line("l_h")
        l_sx = line("l_sx")
        l_sh = line("l_sh")
        l_w2 = line("l_w2")
        l_y = line("l_y")
        l_cum = line("l_cum")
        ctxn_free = [None]

        def post_gen(b, ctx_ready):
            xg = view(scr[:, 0:1], 0, [[256, 4], [1, 256]])
            hg = view(scr[:, 0:1], 1024, [[256, 4], [1, 256]])
            h2T = view(scr[:, 0:1], 2048, [[512, 2], [1, 512]])
            act = view(scr[:, 0:1], 3072, [[512, 4], [1, 512]])
            phase = list(scr_free)
            sx = sh = xg_rd = None
            for blk in range(4):
                ld = SP.dma(l_a, xg, xT_v[b, blk], *phase, sx, xg_rd)
                r = rstd(lambda i: ctxn[:, 4 * blk + i, :], ctx_ready)
                yield
                yield
                n = normalize(lambda i: ctxn[:, 4 * blk + i, :], lambda i: ctxn[:, 4 * blk + i, :], r)
                yield
                xs = DV.op(lambda e, blk=blk: e.tensor_tensor(xg, xg, ctxn[:, 4 * blk:4 * blk + 4, :], ALU.add),
                           ld, n)
                ctxn_free[0] = xs
                yield
                sx = SP.dma(l_sx, X1v[4 * b + blk], xg, xs)
                r = rstd(lambda i: xg[:, i, :], xs)
                yield
                yield
                n = normalize(lambda i: hg[:, i, :], lambda i: xg[:, i, :], r, sh, *phase)
                xg_rd = n
                sh = SP.dma(l_sh, XHv[4 * b + blk][:, :, 0:C], hg, n)
                yield
            done_x = l_sx.done()
            hfree = None
            tfree = None
            for blk in range(4):
                ld = SP.dma(l_h, hg, XHv[4 * b + blk][:, :, 0:C], l_sh.done(), hfree)
                yield
                yield
                bk2 = [next_bank(), next_bank()]
                p = transposes(bk2, lambda i: hg[:, i, :], ld)
                hfree = p
                yield
                e0 = DV.op(lambda e: e.tensor_copy(h2T[:, 0, :], ps[bk2[0]][:, :]), p, tfree, *phase)
                e1 = AC.op(lambda e: e.activation(h2T[:, 1, :], ps[bk2[1]][:, :], ACT.Copy), p, tfree, *phase)
                bank_free[bk2[0]], bank_free[bk2[1]] = e0, e1
                yield
                k = next_bank()
                for i in range(4):
                    for c in range(2):
                        p = PE.op(lambda e, k=k, i=i, c=c: e.matmul(
                            ps[k][:, 65 * i:65 * i + 65], h2T[:, c, 128 * i:128 * i + 128], wg_sb[:, c, :],
                            start=(c == 0), stop=(c == 1)), *take(k, e0, e1, wf_ready), inc=(i == 3 and c == 1))
                tfree = p
                lg = DV.op(lambda e, k=k, blk=blk: e.tensor_copy(
                    Lg[:, 4 * blk:4 * blk + 4, :], view(ps[k][:, 0:1], 0, [[65, 4], [1, 65]])), p, *phase)
                bank_free[k] = lg
                yield
            w_tok = None
            g_free = None
            for blk in range(4):
                R4 = view(scr[:, 0:1], 3072, [[64, 4], [1, 64]])
                M4 = view(scr[:, 0:1], 3072 + 256, [[64, 4], [1, 64]])
                E4 = view(scr[:, 0:1], 3072 + 512, [[65, 4], [1, 65]])
                W4 = view(scr[:, 0:1], 3072 + 832, [[64, 4], [1, 64]])
                mx = view(scr[:, 0:1], 3072 + 1088, [[8, 4], [1, 8]])
                sm = view(scr[:, 0:1], 3072 + 1120, [[1, 4]])
                sg4 = view(scr[:, 0:1], 3072 + 1124, [[1, 4]])
                cm = view(scr[0:NE, 0:1], 3072 + 1136, [[1, 512]])
                L4 = Lg[:, 4 * blk:4 * blk + 4, 0:NE]
                for i in range(4):
                    a = DV.op(lambda e, i=i, blk=blk: e.max(mx[:, i, :], Lg[:, 4 * blk + i, 0:NE]), lg, g_free)
                yield
                for i in range(4):
                    a2 = DV.op(lambda e, i=i, blk=blk: e.match_replace(
                        out=R4[:, i, :], in_to_replace=mx[:, i, :], in_values=Lg[:, 4 * blk + i, 0:NE],
                        imm_value=-3.0e38), a, g_free)
                yield
                mk = DV.op(lambda e, L4=L4: e.tensor_tensor(M4, R4, L4, ALU.not_equal), a2, g_free)
                d = DV.op(lambda e, L4=L4: e.tensor_tensor(E4[:, :, 0:64], L4, view(mx, 0, [[8, 4], [0, 64]]),
                                                           ALU.subtract), a)
                d2 = DV.op(lambda e, blk=blk: e.tensor_scalar(E4[:, :, 64:65], Lg[:, 4 * blk:4 * blk + 4, 64:65],
                                                              -1.0, None, ALU.mult))
                yield
                ex = AC.op(lambda e: e.activation(E4, E4, ACT.Exp), d2)
                k = next_bank()
                for i in range(4):
                    pt = PE.op(lambda e, k=k, i=i: e.transpose(ps[k][0:NE, 128 * i:128 * i + 128], M4[:, i, :],
                                                               ident[:, :]), *take(k, mk), inc=(i == 3))
                yield
                a = DV.op(lambda e: e.tensor_tensor(W4, E4[:, :, 0:64], M4, ALU.mult), ex, w_tok)
                a = DV.op(lambda e: e.tensor_reduce(sm, W4, AX.X, ALU.add), a)
                a = DV.op(lambda e: e.reciprocal(sm, sm), a)
                wn = DV.op(lambda e: e.tensor_tensor(W4, W4, view(sm, 0, [[1, 4], [0, 64]]), ALU.mult), a)
                w_tok = SP.dma(l_w2, XHv[4 * b + blk][:, :, C:C + NE], W4, wn)
                yield
                a = DV.op(lambda e: e.tensor_scalar(sg4, E4[:, :, 64], 1.0, None, ALU.add))
                sgt = DV.op(lambda e, blk=blk: e.reciprocal(sg[:, 4 * blk:4 * blk + 4], sg4), a)
                zr = DV.op(lambda e: e.memset(view(scr[0:NE, 0:1], 2048, [[1, 512]]), 0.0), tfree)
                sc = DV.op(lambda e, k=k: e.tensor_tensor_scan(
                    cm, ps[k][0:NE, :], view(scr[0:NE, 0:1], 2048, [[1, 512]]), carry[:, :], ALU.add, ALU.add),
                    pt, zr, l_cum.done())
                bank_free[k] = sc
                cy = DV.op(lambda e: e.tensor_copy(carry[:, :], cm[:, 511:512]), sc)
                cb = DV.op(lambda e, b=b, blk=blk: e.tensor_copy(
                    bs[:, 16 * b + 4 * blk:16 * b + 4 * blk + 4], view(cm, 127, [[128, 4]])))
                SP.dma(l_cum, CUM[:, 16 * b + 4 * blk:16 * b + 4 * blk + 4, :].rearrange("e i t -> e (i t)"), cm, sc)
                g_free = cb
                yield
            y_tok = None
            yfree = None
            act_free = None
            for blk in range(4):
                ld = SP.dma(l_h, hg, XHv[4 * b + blk][:, :, 0:C], hfree)
                yield
                yield
                bk2 = [next_bank(), next_bank()]
                p = transposes(bk2, lambda i: hg[:, i, :], ld)
                hfree = p
                yield
                e0 = DV.op(lambda e: e.tensor_copy(h2T[:, 0, :], ps[bk2[0]][:, :]), p, tfree, g_free)
                e1 = AC.op(lambda e: e.activation(h2T[:, 1, :], ps[bk2[1]][:, :], ACT.Copy), p, tfree, g_free)
                bank_free[bk2[0]], bank_free[bk2[1]] = e0, e1
                yield
                for m in range(4):
                    kg, ku = next_bank(), next_bank()
                    for k, o in ((kg, 128 * m), (ku, NS + 128 * m)):
                        for c in range(2):
                            p = PE.op(lambda e, k=k, o=o, c=c: e.matmul(
                                ps[k][:, :], wsgu[:, c, o:o + 128], h2T[:, c, :], start=(c == 0), stop=(c == 1)),
                                *take(k, e0, e1), inc=(c == 1))
                        yield
                    s1 = AC.op(lambda e, kg=kg, m=m: e.activation(act[:, m, :], ps[kg][:, :], ACT.Silu), p,
                               act_free, w_tok, l_cum.done(), g_free)
                    bank_free[kg] = s1
                    s2 = DV.op(lambda e, ku=ku, m=m: e.tensor_tensor(act[:, m, :], act[:, m, :], ps[ku][:, :],
                                                                     ALU.mult), s1)
                    bank_free[ku] = s2
                    yield
                tfree = p
                for pair in range(2):
                    k = next_bank()
                    for i in range(2):
                        ti = 2 * pair + i
                        for m in range(4):
                            p = PE.op(lambda e, k=k, i=i, ti=ti, m=m: e.matmul(
                                ps[k][:, 256 * i:256 * i + 256], act[:, m, 128 * ti:128 * ti + 128],
                                wsdn[:, m, :], start=(m == 0), stop=(m == 3)), *take(k, s2),
                                inc=(i == 1 and m == 3))
                        yield
                    for i in range(2):
                        ti = 2 * pair + i
                        ya = AC.op(lambda e, k=k, i=i, ti=ti, blk=blk: e.activation(
                            xg[:, ti, :], ps[k][:, 256 * i:256 * i + 256], ACT.Copy,
                            scale=sg[:, 4 * blk + ti:4 * blk + ti + 1]), p, sgt, y_tok, done_x)
                    bank_free[k] = ya
                    yield
                act_free = p
                y_tok = SP.dma(l_y, Yv[4 * b + blk], xg, ya)
            scr_free[:] = [y_tok, PE.last(), DV.last(), w_tok, l_cum.done(), l_sx.done(), l_sh.done()]
            yield

        l_zb = [line(f"l_zb{i}") for i in range(NZB)]
        zb_free = [None] * NZB
        tb_free = [None] * NTB
        zb_tok = {}
        heads = [(b, g) for b in range(NB) for g in range(H)]

        def load_zb(n):
            b, g = heads[n]
            s = n % NZB
            src = bass.AP(ZQ.tensor, ZQ[b].offset + g * 128, [[0, 128], [H * 128, H], [1, 128]])
            zb_tok[n] = SP.dma(l_zb[s], ZB[:, s * NT:(s + 1) * NT].rearrange("p (h u) -> p h u", u=128), src,
                               zb_free[s], front[b][0])

        def run(gen, steps):
            for _ in range(steps):
                try:
                    next(gen)
                except StopIteration:
                    return

        def chain(*gens):
            for g in gens:
                yield from g

        def quad_out(b, q, ready):
            for t4 in range(8):
                k = 7
                for i in range(2):
                    p = PE.op(lambda e, k=k, i=i, t4=t4: e.transpose(
                        ps[k][:, 128 * i:128 * i + 128], ctxT[:, 128 * (2 * t4 + i):128 * (2 * t4 + i) + 128],
                        ident[:, :]), *take(k, ready), inc=(i == 1))
                c = DV.op(lambda e, k=k, t4=t4, q=q: e.tensor_tensor(
                    view(ctxn[:, 0, 0:1], 2 * t4 * C + 64 * q, [[C, 2], [16, 4], [1, 16]]),
                    view(ps[k][:, 0:1], 0, [[128, 2], [32, 4], [1, 16]]),
                    view(sB[:, 4 * q:4 * q + 1], 0, [[0, 2], [1, 4], [0, 16]]), ALU.mult),
                    p, sB_ready, ctxn_free[0])
                bank_free[k] = c
                quad_done[0] = p
                ctx_tok[0] = c
                yield

        quad_done = [None]
        ctx_tok = [None]
        tcount = [0]

        def attention(b, bg):
            zq, v_done, nz = front[b]
            par = b % 2
            qg = iter(())
            for q in range(4):
                base = b * H + 4 * q
                for j in range(4):
                    if base + j not in zb_tok:
                        load_zb(base + j)
                for kb in range(KB):
                    ts = []
                    for j in range(4):
                        n = base + j
                        g = 4 * q + j
                        s = n % NZB
                        tb = tcount[0] % NTB
                        tcount[0] += 1
                        T = TB[:, tb * NT:(tb + 1) * NT]
                        col = kb * H + g
                        a = AC.op(lambda e, T=T, s=s, col=col, par=par: e.activation(
                            T, ZB[:, s * NT:(s + 1) * NT], ACT.Abs, bias=nzk[par][:, col:col + 1], scale=1.0),
                            zb_tok[n], tb_free[tb], nz)
                        if kb == KB - 1:
                            zb_free[s] = a
                            if n + NZB < len(heads) and heads[n + NZB][0] in front:
                                load_zb(n + NZB)
                        m = DV.op(lambda e, T=T, g=g: e.tensor_scalar(T, T, bb[:, g:g + 1], bb[:, g:g + 1],
                                                                      ALU.min, ALU.subtract), a, b_ready)
                        ts.append((T, m, tb))
                        run(qg, 1)
                        run(bg, 1)
                    for nn in range(4):
                        for j in range(4):
                            T, m, tb = ts[j]
                            g = 4 * q + j
                            o = kb * C + g * D
                            p = PE.op(lambda e, T=T, nn=nn, j=j, o=o, kb=kb, par=par: e.matmul(
                                ps[nn][32 * j:32 * j + 32, :], V[par][:, o:o + 32],
                                T[:, 512 * nn:512 * nn + 512], start=(kb == 0), stop=(kb == KB - 1)),
                                m, v_done, bank_free[nn], inc=(j == 3))
                        if kb == KB - 1:
                            if nn % 2:
                                c = AC.op(lambda e, nn=nn: e.activation(
                                    ctxT[:, 512 * nn:512 * nn + 512], ps[nn][:, :], ACT.Copy), p, quad_done[0])
                                evA = c
                            else:
                                c = DV.op(lambda e, nn=nn: e.tensor_copy(
                                    ctxT[:, 512 * nn:512 * nn + 512], ps[nn][:, :]), p, quad_done[0])
                                evD = c
                            bank_free[nn] = c
                    for _, _, tb in ts:
                        tb_free[tb] = p
                run(qg, 1000)
                qg = both(quad_out(b, q, None), evA, evD, b, q)
            V_free[par] = p
            run(qg, 1000)
            run(bg, 100000)

        def both(_, evA, evD, b, q):
            PE.wait(evA, evD)
            yield from quad_out(b, q, evA)

        run(front_gen(0), 100000)
        for b in range(NB):
            gens = []
            if b:
                gens.append(post_gen(b - 1, ctx_tok[0]))
            if b + 1 < NB:
                gens.append(front_gen(b + 1))
            attention(b, chain(*gens))
        run(post_gen(NB - 1, ctx_tok[0]), 100000)

        rot_all = [0]

        def any_bank():
            k = rot_all[0]
            rot_all[0] = (k + 1) % 8
            return k

        att_end = [PE.last(), AC.last(), DV.last()]
        l_bs = line("l_bs")
        l_bb = line("l_bb")
        BB = ZB[:, 0:NE * NTILE]
        MB = TB[:, 0:NE * NTILE]
        tau = view(Lg[:, 0, 0:1], 0, [[1, NE]])
        tac = view(Lg[:, 0, 0:1], 64, [[1, NE]])
        off = view(Lg[:, 0, 0:1], 128, [[1, NE]])
        tok = view(Lg[:, 0, 0:1], 192, [[1, NE]])
        e64 = view(Lg[:, 0, 0:1], 256, [[1, NE]])
        over = view(Lg[:, 0, 0:1], 320, [[1, NE]])
        fi = view(Lg[:, 0, 0:1], 384, [[1, NE]])
        idx1 = sb("idx1", [128, NE], i32)
        idx2 = sb("idx2", [128, NE], i32)
        e64i = sb("e64i", [128, NE], i32)
        t = SP.dma(l_bs, BASE.rearrange("a (e i) -> (a e) i", i=NTILE), bs[:, :], DV.last())
        t = SP.dma(l_bb, BB, bass.AP(BASE.tensor, BASE.offset, [[0, 128], [1, NE * NTILE]]), t, *att_end)
        a = PL.op(lambda e: e.iota(e64i[:, :], pattern=[[NTILE, NE]], base=0, channel_multiplier=0))
        a = PL.op(lambda e: e.tensor_copy(e64, e64i[:, :]), a, *att_end)
        m = DV.op(lambda e: e.tensor_scalar(MB, BB, scol[:, 0:1], None, ALU.is_le), t, s_ready, *att_end)
        m = DV.op(lambda e: e.tensor_reduce(tau, view(MB, 0, [[NTILE, NE], [1, NTILE]]), AX.X, ALU.add), m)
        m2 = DV.op(lambda e: e.tensor_scalar(tac, tau, float(NTILE - 1), None, ALU.min), m)
        m3 = DV.op(lambda e: e.tensor_scalar(over, tau, float(NTILE) - 0.5, scol[:, 0:1], ALU.is_gt, ALU.mult))
        m4 = DV.op(lambda e: e.tensor_tensor(fi, tac, e64, ALU.add), m2, a)
        i1 = DV.op(lambda e: e.tensor_copy(idx1[:, :], fi), m4)
        m5 = DV.op(lambda e: e.tensor_scalar(tac, tac, 128.0, None, ALU.mult), m4)

        GN = 16
        GR = view(TB[:, 4096:4097], 0, [[128, GN], [1, 128]])
        GC = view(TB[:, 6144:6145], 0, [[128, GN], [1, 128]])
        cum_rows = CUM.rearrange("e i t -> (e i) t")
        l_g = line("l_g")
        idx_ready = []
        gc = None
        for grp in range(NE // GN):
            for i in range(GN):
                e_ = grp * GN + i
                gt = PL.transfer(l_g, lambda e: e.indirect_dma_start(
                    GR[:, i, :], None, cum_rows,
                    bass.IndirectOffsetOnAxis(ap=idx1[:, e_:e_ + 1].bitcast(u32), axis=0)),
                    i1, l_cum.done(), gc)
            gc = DV.op(lambda e: e.tensor_scalar(GC, GR, scol[:, 0:1], None, ALU.is_le), gt)
            r = DV.op(lambda e, grp=grp: e.tensor_reduce(off[:, grp * GN:(grp + 1) * GN], GC, AX.X, ALU.add), gc)
            sl = slice(grp * GN, (grp + 1) * GN)
            r = DV.op(lambda e, sl=sl: e.tensor_tensor(tok[:, sl], off[:, sl], tac[:, sl], ALU.add), r, m5)
            r = DV.op(lambda e, sl=sl: e.tensor_tensor(fi[:, sl], tok[:, sl], over[:, sl], ALU.add), r, m3)
            r = DV.op(lambda e, sl=sl: e.tensor_copy(idx2[:, sl], fi[:, sl]), r)
            idx_ready.append(r)

        NX = 4
        W0 = 8192
        l_ew = [line(f"l_ew{i}") for i in range(NX)]
        l_xe = [line(f"l_xe{i}") for i in range(NX)]
        l_sc = line("l_sc")
        ZO = 4096
        wgu = [view(ZB[:, ZO:ZO + 1], 768 * i, [[256, 2], [1, 256]]) for i in range(NX)]
        wdn = [view(ZB[:, ZO:ZO + 1], 768 * i + 512, [[1, 256]]) for i in range(NX)]
        xe = [view(TB[:, W0:W0 + 1], 320 * i, [[1, 320]]) for i in range(NX)]
        ye = [view(TB[:, W0:W0 + 1], 1280 + 256 * i, [[1, 256]]) for i in range(NX)]
        xeT = [view(TB[:, W0:W0 + 1], 2304 + 256 * i, [[128, 2], [1, 128]]) for i in range(2)]
        ae = [view(TB[:, W0:W0 + 1], 2816 + 128 * i, [[1, 128]]) for i in range(2)]
        w_free, x_free, xT_free, a_free, y_free = [None] * NX, [None] * NX, [None] * 2, [None] * 2, [None] * NX
        ew, xt = {}, {}

        def load_expert(n):
            s = n % NX
            SP.dma(l_ew[s], wgu[s], egu_w[n].rearrange("(k p) f -> p k f", p=128), w_free[s], *att_end)
            ew[n] = SP.dma(l_ew[s], wdn[s], edn_w[n], w_free[s])

        def gather_expert(n):
            s = n % NX
            xt[n] = PL.transfer(l_xe[s], lambda e: e.indirect_dma_start(
                xe[s], None, XH, bass.IndirectOffsetOnAxis(ap=idx2[:, n:n + 1].bitcast(u32), axis=0)),
                idx_ready[n // GN], x_free[s], l_w2.done(), l_sh.done(), zero_sent)

        for n in range(NX - 1):
            load_expert(n)
            gather_expert(n)
        sc_tok = None
        for n in range(NE):
            if n + NX - 1 < NE:
                load_expert(n + NX - 1)
                gather_expert(n + NX - 1)
            s, s2 = n % NX, n % 2
            k = any_bank()
            for c in range(2):
                p = PE.op(lambda e, k=k, c=c, s=s: e.transpose(ps[k][:, 128 * c:128 * c + 128],
                                                               xe[s][:, 128 * c:128 * c + 128], ident[:, :]),
                          *take(k, xt[n]), inc=(c == 1))
            v = DV.op(lambda e, k=k, s2=s2: e.tensor_copy(xeT[s2], view(ps[k][:, 0:1], 0, [[128, 2], [1, 128]])),
                      p, xT_free[s2])
            bank_free[k] = v
            k = any_bank()
            for f in range(2):
                for c in range(2):
                    p = PE.op(lambda e, k=k, f=f, c=c, s=s, s2=s2: e.matmul(
                        ps[k][:, 128 * f:128 * f + 128], wgu[s][:, c, 128 * f:128 * f + 128], xeT[s2][:, c, :],
                        start=(c == 0), stop=(c == 1)), *take(k, v, ew[n]), inc=(f == 1 and c == 1))
            xT_free[s2] = p
            a = AC.op(lambda e, k=k, s2=s2: e.activation(ae[s2], ps[k][:, 0:128], ACT.Silu), p, a_free[s2])
            v = DV.op(lambda e, k=k, s2=s2: e.tensor_tensor(ae[s2], ae[s2], ps[k][:, 128:256], ALU.mult), a)
            bank_free[k] = v
            k = any_bank()
            p = PE.op(lambda e, k=k, s=s, s2=s2: e.matmul(ps[k][:, 0:256], ae[s2], wdn[s], start=True, stop=True),
                      *take(k, v))
            a_free[s2] = p
            w_free[s] = p
            a = AC.op(lambda e, k=k, s=s, n=n: e.activation(ye[s], ps[k][:, 0:256], ACT.Copy,
                                                            scale=xe[s][:, C + n:C + n + 1]), p, y_free[s])
            bank_free[k] = a
            x_free[s] = a
            sc_tok = PL.transfer(l_sc, lambda e: e.indirect_dma_start(
                Y, bass.IndirectOffsetOnAxis(ap=idx2[:, n:n + 1].bitcast(u32), axis=0), ye[s], None,
                compute_op=ALU.add), a, sc_tok, l_y.done(), zero_sent)
            y_free[s] = sc_tok

        NF = 4
        l_fy = [line(f"l_fy{i}") for i in range(NF)]
        l_fx = [line(f"l_fx{i}") for i in range(NF)]
        l_o = [line(f"l_o{i}") for i in range(NF)]
        yt = [view(ZB[:, 0:1], 1024 * i, [[256, 4], [1, 256]]) for i in range(NF)]
        x1t = [view(TB[:, 0:1], 1024 * i, [[256, 4], [1, 256]]) for i in range(NF)]
        endt = [PE.last(), DV.last(), AC.last()]
        for n in range(NTILE // 4):
            s = n % NF
            ly = SP.dma(l_fy[s], yt[s], Yv[n], sc_tok, l_o[s].done(), *endt)
            lx = SP.dma(l_fx[s], x1t[s], X1v[n], l_sx.done(), l_o[s].done())
            r = rstd(lambda i, s=s: yt[s][:, i, :], ly)
            v = normalize(lambda i, s=s: yt[s][:, i, :], lambda i, s=s: yt[s][:, i, :], r)
            v = DV.op(lambda e, s=s: e.tensor_tensor(yt[s], yt[s], x1t[s], ALU.add), v, lx)
            SP.dma(l_o[s], outv[n], yt[s], v)
        SP.wait(*[l.done() for l in l_o], l_sc.done(), l_y.done(), l_zero.done(), l_bs.done(), l_cum.done(),
              l_w2.done(), l_sh.done(), l_sx.done(), l_zq.done())


_A = 'L0_attn_'
_F = 'L0_ffn_'


def kernel(**inputs):
    import numpy as _np
    import concourse.bacc as _bacc
    from concourse import mybir as _mybir
    from concourse.bass_utils import run_bass_kernel_spmd as _run

    g = lambda n: _np.asarray(inputs[n])
    lay = {
        "x": g(_A + 'hidden_states'),
        "WqT": g(_A + 'Wq').T, "bq": g(_A + 'bq').reshape(2, 128).T,
        "WkT": g(_A + 'Wk').T, "bk": g(_A + 'bk').reshape(2, 128).T,
        "WvT": g(_A + 'Wv').T, "bv": g(_A + 'bv'),
        "WpT": g(_A + 'Wproj').reshape(16, 16, 16).transpose(2, 1, 0),
        "lbw": g(_A + 'log_bandwidth'),
        "gates_w": _np.concatenate([g(_F + 'gate_w'), g(_F + 'shared_gate_w')], axis=1),
        "sgu_w": g(_F + 'shared_gate_up_w'), "sdn_w": g(_F + 'shared_down_w'),
        "egu_w": g(_F + 'expert_gate_up_w'), "edn_w": g(_F + 'expert_down_w'),
    }
    nc = _bacc.Bacc("TRN2", target_bir_lowering=False, num_devices=1)
    arrays, args = {}, []
    for n, a in lay.items():
        a = _np.ascontiguousarray(a)
        arrays["in_" + n] = a
        args.append(nc.dram_tensor("in_" + n, a.shape, _mybir.dt.from_np(a.dtype), kind="ExternalInput").ap())
    out = nc.dram_tensor("out_0", (4, 2048, 256), _mybir.dt.float32, kind="ExternalOutput").ap()
    build(nc, *args, out)
    r = _run(nc, [arrays], core_ids=[0])
    return r.results[0]["out_0"]
```

```python
import concourse.bass as bass
from concourse import mybir
from contextlib import ExitStack

fp32 = mybir.dt.float32
u32 = mybir.dt.uint32
i32 = mybir.dt.int32
ALU = mybir.AluOpType
ACT = mybir.ActivationFunctionType
AX = mybir.AxisListType

NB, NT, C, H, D = 4, 2048, 256, 16, 16
KB = NT // 128
NE, CAP, TOPK = 64, 128, 8
NI, NS = 128, 512
TOK = NB * NT
NTILE = TOK // 128
NZB = 5
NCH = 3
NTB = 8
VW = KB * C + 16


class Stream:

    def __init__(self, eng, sem):
        self.eng, self.sem, self.n, self.reached = eng, sem, 0, {}

    def wait(self, *after):
        for t in after:
            if t is not None and t[1] > self.reached.get(id(t[0]), 0):
                self.eng.wait_ge(t[0], t[1])
                self.reached[id(t[0])] = t[1]

    def op(self, fn, *after, inc=True):
        self.wait(*after)
        ins = fn(self.eng)
        if inc:
            ins.then_inc(self.sem, 1)
            self.n += 1
        return (self.sem, self.n)

    def transfer(self, line, fn, *after):
        self.wait(*after)
        fn(self.eng).then_inc(line.sem, 16)
        line.n += 16
        return (line.sem, line.n)

    def dma(self, line, out, in_, *after):
        return self.transfer(line, lambda e: e.dma_start(out, in_), *after)

    def last(self):
        return (self.sem, self.n)


class Line:

    def __init__(self, sem):
        self.sem, self.n = sem, 0

    def done(self):
        return (self.sem, self.n) if self.n else None


def view(a, offset, dims):
    return bass.AP(a.tensor, a.offset + offset, [list(a.ap[0])] + [list(d) for d in dims])


def build(nc, x, WqT, bq, WkT, bk, WvT, bv, WpT, lbw, gates_w, sgu_w, sdn_w, egu_w, edn_w, out):
    with ExitStack() as ctx:
        def sb(name, shape, dt=fp32):
            return ctx.enter_context(nc.sbuf_tensor(name, shape, dt))

        def dram(name, shape):
            return nc.dram_tensor(name, shape, fp32, kind="Internal").ap()

        def line(name):
            return Line(ctx.enter_context(nc.semaphore(name)))

        PE = Stream(nc.tensor, ctx.enter_context(nc.semaphore("s_pe")))
        AC = Stream(nc.scalar, ctx.enter_context(nc.semaphore("s_act")))
        DV = Stream(nc.vector, ctx.enter_context(nc.semaphore("s_dve")))
        PL = Stream(nc.gpsimd, ctx.enter_context(nc.semaphore("s_pool")))
        SP = Stream(nc.sync, ctx.enter_context(nc.semaphore("s_sp")))

        ZQ = dram("zq_rows", (NB, H, H, 128))
        XH = dram("h_rows", (TOK + 128, C + NE))
        X1 = dram("x1_rows", (TOK, C))
        Y = [dram(f"y_rows{i}", (TOK + 128, C)) for i in range(NCH)]
        CUM = dram("cum_rows", (NE, NTILE, 128))
        BASE = dram("base_row", (1, NE * NTILE))

        TB = sb("TB", [128, NTB * NT])
        ZB = sb("ZB", [128, NZB * NT])
        V = [sb(f"V{i}", [128, VW]) for i in range(2)]
        ctxn = sb("ctxn", [128, KB, C])
        scr = sb("scr", [128, 4096])
        BD = sb("BD", [128, 16, 128])
        wq_sb = sb("wq_sb", [128, 2, C])
        wk_sb = sb("wk_sb", [128, 2, C])
        wv_sb = sb("wv_sb", [128, 2, C])
        wg_sb = sb("wg_sb", [128, 2, NE + 1])
        wsgu = sb("wsgu", [128, 2, 2 * NS])
        wsdn = sb("wsdn", [128, 4, C])
        bqc = sb("bqc", [128, 2])
        bkc = sb("bkc", [128, 2])
        bvb = sb("bvb", [128, C])
        ident = sb("ident", [128, 128])
        bb = sb("bb", [128, H])
        bt = sb("bt", [128, 3, H])
        sB = sb("sB", [128, H])
        nzk = [sb(f"nzk{i}", [128, C]) for i in range(2)]
        mhalf = sb("mhalf", [128, 4])
        st6 = [sb(f"st6{i}", [128, 4, 6]) for i in range(4)]
        mv = [sb(f"mv{i}", [128, 4, 2]) for i in range(4)]
        ve = [sb(f"ve{i}", [128, 4]) for i in range(4)]
        rs = [sb(f"rs{i}", [128, 4]) for i in range(4)]
        zero = sb("zero", [128, 320])
        Lg = sb("Lg", [128, KB, NE + 1])
        sg = sb("sg", [128, KB])
        carry = sb("carry", [NE, 1])
        bs = sb("bs", [NE, NTILE])

        scol = sb("scol", [128, 1])
        scoli = sb("scoli", [128, 1], i32)

        ps = [ctx.enter_context(nc.psum_tensor(f"ps{i}", [128, 512], fp32)) for i in range(8)]
        bank_free = [None] * 8

        xT_v = x.rearrange("b (k i p) c -> b k p i c", p=128, i=4)
        X1v = X1.rearrange("(n i p) c -> n p i c", p=128, i=4)
        XHv = XH[0:TOK, :].rearrange("(n i p) c -> n p i c", p=128, i=4)
        Yv = [y_[0:TOK, :].rearrange("(n i p) c -> n p i c", p=128, i=4) for y_ in Y]
        outv = out.rearrange("b (k i p) c -> (b k) p i c", p=128, i=4)

        l_w = line("l_w")
        l_zero = line("l_zero")
        l_sgu = line("l_sgu")
        for dst, src in ((wq_sb, WqT), (wk_sb, WkT), (wv_sb, WvT)):
            SP.dma(l_w, dst[:, :, :], src.rearrange("(k p) n -> p k n", p=128))
        for dst, src in ((bqc, bq), (bkc, bk)):
            SP.dma(l_w, dst[:, :], src)
        SP.dma(l_w, bvb[:, :], bass.AP(bv.tensor, bv.offset, [[0, 128], [1, C]]))
        SP.dma(l_w, bb[:, :], bass.AP(lbw.tensor, lbw.offset, [[0, 128], [1, H]]))
        bd0 = PL.op(lambda e: e.memset(BD[:, :, :], 0.0))
        w_ready = None
        for h in range(8):
            w_ready = SP.dma(l_w, BD[16 * h:16 * h + 16, :, 16 * h:16 * h + 16], WpT, bd0)
        SP.dma(l_sgu, wg_sb[:, :, :], gates_w.rearrange("(k p) n -> p k n", p=128))
        SP.dma(l_sgu, wsgu[:, :, :], sgu_w.rearrange("(k p) n -> p k n", p=128))
        wf_ready = SP.dma(l_sgu, wsdn[:, :, :], sdn_w.rearrange("(k p) n -> p k n", p=128))

        i0 = PL.op(lambda e: e.memset(ident[:, :], 0.0))
        id_ready = PL.op(lambda e: e.affine_select(out=ident[:, :], in_=ident[:, :], compare_op=ALU.not_equal,
                                                   fill=1.0, base=0, pattern=[[-1, 128]], channel_multiplier=1), i0)
        mh_ready = PL.op(lambda e: e.memset(mhalf[:, :], -0.5))
        io = PL.op(lambda e: e.iota(scoli[:, :], pattern=[[0, 1]], base=0, channel_multiplier=1))
        s_ready = PL.op(lambda e: e.tensor_copy(scol[:, :], scoli[:, :]), io)
        carry_tok = [DV.op(lambda e: e.memset(carry[:, :], 0.0))]
        for i in range(2):
            v_pad = DV.op(lambda e, i=i: e.memset(V[i][:, KB * C:VW], 0.0))
        z_ready = DV.op(lambda e: e.memset(zero[:, :], 0.0))
        SP.dma(l_zero, XH[TOK:TOK + 128, :], zero[:, 0:C + NE], z_ready)
        zero_sent = SP.dma(l_zero, Y[0][TOK:TOK + 128, :], zero[:, 0:C])

        t = AC.op(lambda e: e.activation(bt[:, 0, :], bb[:, :], ACT.Abs), w_ready)
        t = AC.op(lambda e: e.activation(bt[:, 1, :], bt[:, 0, :], ACT.Exp, scale=-1.0), t)
        t = AC.op(lambda e: e.activation(bt[:, 2, :], bt[:, 1, :], ACT.Ln, bias=1.0), t)
        t1 = DV.op(lambda e: e.tensor_scalar(bt[:, 0, :], bb[:, :], 0.0, None, ALU.max), t)
        t2 = DV.op(lambda e: e.tensor_tensor(bt[:, 1, :], bt[:, 0, :], bt[:, 2, :], ALU.add), t1)
        b_ready = DV.op(lambda e: e.tensor_scalar(bb[:, :], bt[:, 1, :], 1e-4, None, ALU.add), t2)
        t3 = DV.op(lambda e: e.tensor_scalar(bt[:, 0, :], bb[:, :], -float(NT), None, ALU.mult), b_ready)
        sB_ready = DV.op(lambda e: e.reciprocal(sB[:, :], bt[:, 0, :]), t3)

        def take(bank, *after):
            return [bank_free[bank], *after]

        rot = [4]

        def next_bank():
            k = rot[0]
            rot[0] = 4 + (k - 3) % 3
            return k

        ln_free = [None] * 4

        def rstd(s, ap4, *after):
            for i in range(4):
                a = DV.op(lambda e: e.bn_stats(st6[s][:, i, :], ap4(i)), *after, ln_free[s], inc=(i == 3))
            for i in range(4):
                m = DV.op(lambda e: e.bn_aggr(mv[s][:, i, :], st6[s][:, i, :]), a, inc=(i == 3))
            p = PL.op(lambda e: e.tensor_scalar(ve[s][:, :], view(mv[s][:, 0, 1:2], 0, [[2, 4]]), 1e-5, None,
                                                ALU.add), m)
            return PL.op(lambda e: e.tensor_tensor(rs[s][:, :], ve[s][:, :], mhalf[:, 0:4], ALU.pow), p, mh_ready)

        def normalize(s, dst4, src4, *ready):
            for i in range(4):
                n = DV.op(lambda e: e.tensor_scalar(dst4(i), src4(i), mv[s][:, i, 0:1], rs[s][:, i:i + 1],
                                                    ALU.subtract, ALU.mult), *ready, inc=(i == 3))
            ln_free[s] = n
            return n

        def evac(on_dve, act_fn, dve_fn, *after):
            return DV.op(dve_fn, *after) if on_dve else AC.op(act_fn, *after)

        def transposes(dst_banks, src4, ready):
            for c in range(2):
                for i in range(4):
                    p = PE.op(lambda e, c=c, i=i: e.transpose(ps[dst_banks[c]][:, 128 * i:128 * i + 128],
                                                              src4(i)[:, 128 * c:128 * c + 128], ident[:, :]),
                              *take(dst_banks[c], ready, id_ready), inc=(i == 3))
            return p

        l_x = [line(f"l_x{i}") for i in range(4)]
        l_zq = line("l_zq")
        front = {}
        scr_free = [zero_sent]
        V_free = [None, None]

        def front_gen(b):
            par = b % 2
            if b:
                xg = [view(scr[:, 0:1], 0, [[256, 4], [1, 256]])] * 4
            else:
                xg = [ctxn[:, 4 * i:4 * i + 4, :] for i in range(4)]
            hT = view(scr[:, 0:1], 1024, [[1024, 2], [1, 1024]])
            QK = view(scr[:, 0:1], 3072, [[1, 1024]])
            Zs = view(Lg[:, 0, 0:1], 0, [[256, 2], [128, 2], [1, 128]])
            phase = list(scr_free)
            hT_free = qk_free = None
            xg_free = [None] * 4
            n_tok = {}

            def rows(blk):
                xa = xg[blk]
                ld = SP.dma(l_x[blk], xa, xT_v[b, blk], *phase, xg_free[blk])
                yield
                yield
                yield
                r = rstd(blk, lambda i: xa[:, i, :], ld)
                yield
                yield
                n_tok[blk] = normalize(blk, lambda i: xa[:, i, :], lambda i: xa[:, i, :], r)
                yield

            if b == 0:
                gs = [rows(i) for i in range(4)]
                for _ in range(6):
                    for g_ in gs:
                        next(g_)
            for hf in range(2):
                for g in range(2):
                    blk = 2 * hf + g
                    xa = xg[blk]
                    if b:
                        yield from rows(blk)
                    bk2 = [next_bank(), next_bank()]
                    p = transposes(bk2, lambda i: xa[:, i, :], n_tok[blk])
                    if b and blk < 3:
                        xg_free[blk + 1] = p
                    yield
                    ev0 = DV.op(lambda e: e.tensor_copy(hT[:, 0, 512 * g:512 * g + 512], ps[bk2[0]][:, :]),
                                p, hT_free, *phase)
                    yield
                    ev = evac(b, lambda e: e.activation(hT[:, 1, 512 * g:512 * g + 512], ps[bk2[1]][:, :], ACT.Copy),
                              lambda e: e.tensor_copy(hT[:, 1, 512 * g:512 * g + 512], ps[bk2[1]][:, :]),
                              p, hT_free, *phase)
                    bank_free[bk2[0]], bank_free[bk2[1]] = ev0, ev
                    yield
                    for pair in range(2):
                        k = next_bank()
                        for i in range(2):
                            ti = 2 * pair + i
                            for c in range(2):
                                p = PE.op(lambda e, k=k, i=i, c=c, ti=ti: e.matmul(
                                    ps[k][:, 256 * i:256 * i + 256],
                                    hT[:, c, 512 * g + 128 * ti:512 * g + 128 * ti + 128],
                                    wv_sb[:, c, :], start=(c == 0), stop=(c == 1)),
                                    *take(k, ev, ev0, w_ready), inc=(i == 1 and c == 1))
                        o = (4 * blk + 2 * pair) * C
                        v_done = DV.op(lambda e, k=k, o=o: e.tensor_tensor(
                            view(V[par][:, o:o + 1], 0, [[256, 2], [1, 256]]),
                            view(ps[k][:, 0:1], 0, [[256, 2], [1, 256]]),
                            view(bvb[:, 0:1], 0, [[0, 2], [1, 256]]), ALU.add), p, V_free[par], v_pad)
                        bank_free[k] = v_done
                        yield
                for pj, (w, bias) in enumerate(((wq_sb, bqc), (wk_sb, bkc))):
                    for m in range(2):
                        for n2 in range(2):
                            k = next_bank()
                            for c in range(2):
                                p = PE.op(lambda e, k=k, c=c, n2=n2, m=m, w=w: e.matmul(
                                    ps[k][:, :], w[:, c, 128 * m:128 * m + 128],
                                    hT[:, c, 512 * n2:512 * n2 + 512], start=(c == 0), stop=(c == 1)),
                                    *take(k, ev, ev0, w_ready), inc=(c == 1))
                            q = evac(b and n2 == 0, lambda e: e.activation(
                                QK[:, 512 * n2:512 * n2 + 512], ps[k][:, :], ACT.Identity,
                                bias=bias[:, m:m + 1]),
                                lambda e: e.tensor_scalar(QK[:, 512 * n2:512 * n2 + 512], ps[k][:, :],
                                                          bias[:, m:m + 1], None, ALU.add),
                                p, qk_free, *phase)
                            q0 = q if n2 == 0 else q0
                            bank_free[k] = q
                            yield
                        hT_free = p
                        k = next_bank()
                        for tt in range(16):
                            p = PE.op(lambda e, k=k, tt=tt: e.matmul(
                                ps[k][:, 0:64], BD[:, tt, :], view(QK[:, 0:1], tt, [[16, 64]]),
                                start=(tt == 0), stop=(tt == 15)), *take(k, q0, q), inc=(tt == 15))
                            if tt % 4 == 3:
                                yield
                        qk_free = p
                        zc = DV.op(lambda e, k=k, pj=pj, m=m, hf=hf: e.tensor_copy(
                            Zs[:, pj, m, 64 * hf:64 * hf + 64], ps[k][:, 0:64]), p, *phase)
                        bank_free[k] = zc
                        yield
            zq = None
            for m in range(2):
                dst = bass.AP(ZQ.tensor, ZQ[b].offset + m * 8 * H * 128, [[128, 128], [1, 128]])
                zq = SP.dma(l_zq, dst, Zs[:, 0, m, :], zc)
            k = next_bank()
            for m in range(2):
                p = PE.op(lambda e, k=k, m=m: e.transpose(ps[k][:, 128 * m:128 * m + 128], Zs[:, 1, m, :],
                                                          ident[:, :]), *take(k, zc), inc=(m == 1))
            nz = DV.op(lambda e, k=k: e.tensor_scalar(nzk[par][:, :], ps[k][:, 0:256], -1.0, None, ALU.mult),
                       p, V_free[par])
            bank_free[k] = nz
            scr_free[:] = [PE.last(), nz, AC.last(), zq]
            front[b] = (zq, v_done, nz)
            yield

        l_a = [line(f"l_a{i}") for i in range(4)]
        l_h = line("l_h")
        l_sx = [line(f"l_sx{i}") for i in range(4)]
        l_sh = [line(f"l_sh{i}") for i in range(4)]
        l_w2 = [line(f"l_w2{i}") for i in range(4)]
        l_y = line("l_y")
        l_cum = [line(f"l_cum{i}") for i in range(4)]
        ctxn_free = [None]

        def all_of(lines):
            return [l.done() for l in lines]

        class Room:

            def __init__(self, tail):
                T0 = TB[:, 0:1]
                S0 = scr[:, 0:1]
                if tail:
                    self.x = [view(T0, 1024 * i, [[256, 4], [1, 256]]) for i in range(4)]
                    self.h = [view(T0, 4096 + 1024 * i, [[256, 4], [1, 256]]) for i in range(4)]
                    self.r = [(T0, 8192 + 2048 * i) for i in range(4)]
                else:
                    self.x = [view(S0, 3072, [[256, 4], [1, 256]])] * 4
                    self.h = [view(S0, 0, [[256, 4], [1, 256]])] * 4
                    self.r = [(S0, 2048)] * 4
                self.tail = tail
                self.hT = view(S0, 1024, [[512, 2], [1, 512]])
                self.act = view(S0, 2048, [[512, 4], [1, 512]])
                self.y = view(S0, 0, [[256, 4], [1, 256]])
                self.x_free, self.h_free, self.r_free = [[None] * 4 for _ in range(3)]
                self.h_tok = [None] * 4
                self.hT_free = self.lg = self.sg = None

        def post_rows(b, blk, room, phase, ctx_ready):
            xg, hg = room.x[blk], room.h[blk]
            prev = (blk - 1) % 4
            same = [] if room.tail else [l_sx[prev].done(), room.x_free[prev]]
            ld = SP.dma(l_a[blk], xg, xT_v[b, blk], *phase, *same)
            cx = lambda i: ctxn[:, 4 * blk + i, :]
            r = rstd(blk, cx, ctx_ready)
            yield
            yield
            n = normalize(blk, cx, cx, r)
            yield
            add = lambda e: e.tensor_tensor(xg, xg, ctxn[:, 4 * blk:4 * blk + 4, :], ALU.add)
            xs = (DV if room.tail else PL).op(add, ld, n)
            ctxn_free[0] = xs
            yield
            yield
            SP.dma(l_sx[blk], X1v[4 * b + blk], xg, xs)
            r = rstd(blk, lambda i: xg[:, i, :], xs)
            yield
            yield
            n = normalize(blk, lambda i: hg[:, i, :], lambda i: xg[:, i, :], r, *phase,
                          *([] if room.tail else [l_sh[prev].done()]))
            room.x_free[blk] = room.h_tok[blk] = n
            SP.dma(l_sh[blk], XHv[4 * b + blk][:, :, 0:C], hg, n)
            yield

        def load_hT(b, blk, room, phase, *after):
            hg = room.h[blk]
            if room.tail:
                ld = room.h_tok[blk]
            else:
                ld = SP.dma(l_h, hg, XHv[4 * b + blk][:, :, 0:C], *all_of(l_sh), l_y.done(), room.h_free[0])
                yield
                yield
            bk2 = [next_bank(), next_bank()]
            p = transposes(bk2, lambda i: hg[:, i, :], ld)
            room.h_free[0] = p
            yield
            e0 = DV.op(lambda e: e.tensor_copy(room.hT[:, 0, :], ps[bk2[0]][:, :]), p, room.hT_free, *phase, *after)
            e1 = AC.op(lambda e: e.activation(room.hT[:, 1, :], ps[bk2[1]][:, :], ACT.Copy), p, room.hT_free,
                       *phase, *after)
            bank_free[bk2[0]], bank_free[bk2[1]] = e0, e1
            room.hT_tok = (e0, e1)
            yield

        def post_logits(b, room, phase):
            for blk in range(4):
                yield from load_hT(b, blk, room, phase)
                k = next_bank()
                for i in range(4):
                    for c in range(2):
                        p = PE.op(lambda e: e.matmul(
                            ps[k][:, 65 * i:65 * i + 65], room.hT[:, c, 128 * i:128 * i + 128], wg_sb[:, c, :],
                            start=(c == 0), stop=(c == 1)), *take(k, *room.hT_tok, wf_ready),
                            inc=(i == 3 and c == 1))
                room.hT_free = p
                yield
                room.lg = DV.op(lambda e: e.tensor_copy(
                    Lg[:, 4 * blk:4 * blk + 4, :], view(ps[k][:, 0:1], 0, [[65, 4], [1, 65]])), p, *phase)
                bank_free[k] = room.lg
                yield

        def post_route(b, blk, room):
            base, o = room.r[blk]
            R4 = view(base, o, [[64, 4], [1, 64]])
            M4 = view(base, o + 256, [[64, 4], [1, 64]])
            E4 = view(base, o + 512, [[65, 4], [1, 65]])
            W4 = view(base, o + 832, [[64, 4], [1, 64]])
            mx = view(base, o + 1088, [[8, 4], [1, 8]])
            sm = view(base, o + 1120, [[1, 4]])
            sg4 = view(base, o + 1124, [[1, 4]])
            b64 = scr[0:NE, 0:1] if not room.tail else TB[0:NE, 0:1]
            cm = view(b64, o + 1136, [[1, 512]])
            L4 = Lg[:, 4 * blk:4 * blk + 4, 0:NE]
            prev = (blk - 1) % 4
            free = [] if room.tail else [room.r_free[prev], l_w2[prev].done(), l_cum[prev].done()]
            for i in range(4):
                a = DV.op(lambda e: e.max(mx[:, i, :], Lg[:, 4 * blk + i, 0:NE]), room.lg, *free, inc=(i == 3))
            yield
            for i in range(4):
                a2 = DV.op(lambda e: e.match_replace(
                    out=R4[:, i, :], in_to_replace=mx[:, i, :], in_values=Lg[:, 4 * blk + i, 0:NE],
                    imm_value=-3.0e38), a, inc=(i == 3))
            yield
            d = DV.op(lambda e: e.tensor_tensor(E4[:, :, 0:64], L4, view(mx, 0, [[8, 4], [0, 64]]), ALU.subtract), a)
            d = DV.op(lambda e: e.tensor_scalar(E4[:, :, 64:65], Lg[:, 4 * blk:4 * blk + 4, 64:65],
                                                -1.0, None, ALU.mult))
            mk = DV.op(lambda e: e.tensor_tensor(M4, R4, L4, ALU.not_equal), a2)
            yield
            ex = AC.op(lambda e: e.activation(E4, E4, ACT.Exp), d)
            k = blk if room.tail else next_bank()
            for i in range(4):
                pt = PE.op(lambda e: e.transpose(ps[k][0:NE, 128 * i:128 * i + 128], M4[:, i, :], ident[:, :]),
                           *take(k, mk), inc=(i == 3))
            yield
            sc = DV.op(lambda e: e.tensor_tensor_scan(cm, ps[k][0:NE, :], view(zero[0:NE, 0:1], 0, [[0, 512]]), carry[:, :],
                                                      ALU.add, ALU.add), pt, z_ready, carry_tok[0])
            bank_free[k] = sc
            carry_tok[0] = DV.op(lambda e: e.tensor_copy(carry[:, :], cm[:, 511:512]), sc)
            cb = DV.op(lambda e: e.tensor_copy(bs[:, 16 * b + 4 * blk:16 * b + 4 * blk + 4],
                                               view(cm, 127, [[128, 4]])))
            SP.dma(l_cum[blk], CUM[:, 16 * b + 4 * blk:16 * b + 4 * blk + 4, :].rearrange("e i t -> e (i t)"), cm, cb)
            yield
            a = PL.op(lambda e: e.tensor_tensor(W4, E4[:, :, 0:64], M4, ALU.mult), ex, mk)
            yield
            a = DV.op(lambda e: e.tensor_reduce(sm, W4, AX.X, ALU.add), a)
            a = DV.op(lambda e: e.reciprocal(sm, sm), a)
            g = DV.op(lambda e: e.tensor_scalar(sg4, E4[:, :, 64], 1.0, None, ALU.add))
            room.sg = DV.op(lambda e: e.reciprocal(sg[:, 4 * blk:4 * blk + 4], sg4), g)
            yield
            wn = PL.op(lambda e: e.tensor_tensor(W4, W4, view(sm, 0, [[1, 4], [0, 64]]), ALU.mult), a)
            SP.dma(l_w2[blk], XHv[4 * b + blk][:, :, C:C + NE], W4, wn)
            room.r_free[blk] = room.sg
            yield

        def post_shared(b, room, phase):
            act = room.act
            free = list(phase)
            if not room.tail:
                free += [*all_of(l_w2), *all_of(l_cum), room.r_free[3]]
            act_free = None
            for blk in range(4):
                yield from load_hT(b, blk, room, phase)
                for m in range(4):
                    kg, ku = next_bank(), next_bank()
                    for k, o in ((kg, 128 * m), (ku, NS + 128 * m)):
                        for c in range(2):
                            p = PE.op(lambda e: e.matmul(
                                ps[k][:, :], wsgu[:, c, o:o + 128], room.hT[:, c, :], start=(c == 0), stop=(c == 1)),
                                *take(k, *room.hT_tok, wf_ready), inc=(c == 1))
                        yield
                    s1 = AC.op(lambda e: e.activation(act[:, m, :], ps[kg][:, :], ACT.Silu), p, act_free, *free)
                    bank_free[kg] = s1
                    yield
                    s2 = DV.op(lambda e: e.tensor_tensor(act[:, m, :], act[:, m, :], ps[ku][:, :], ALU.mult), s1)
                    bank_free[ku] = s2
                    yield
                room.hT_free = p
                for pair in range(2):
                    k = next_bank()
                    for i in range(2):
                        ti = 2 * pair + i
                        for m in range(4):
                            p = PE.op(lambda e: e.matmul(
                                ps[k][:, 256 * i:256 * i + 256], act[:, m, 128 * ti:128 * ti + 128],
                                wsdn[:, m, :], start=(m == 0), stop=(m == 3)), *take(k, s2),
                                inc=(i == 1 and m == 3))
                        yield
                    for i in range(2):
                        ti = 2 * pair + i
                        ya = DV.op(lambda e: e.tensor_scalar(
                            room.y[:, ti, :], ps[k][:, 256 * i:256 * i + 256],
                            sg[:, 4 * blk + ti:4 * blk + ti + 1], None, ALU.mult), p, room.sg, l_y.done(), *free)
                    bank_free[k] = ya
                    yield
                act_free = p
                SP.dma(l_y, Yv[0][4 * b + blk], room.y, ya)

        def post_gen(b, ctx_ready):
            room = Room(False)
            phase = list(scr_free)
            for blk in range(4):
                yield from post_rows(b, blk, room, phase, ctx_ready)
            phase = [*phase, *all_of(l_sx), room.x_free[3]]
            yield from post_logits(b, room, phase)
            for blk in range(4):
                yield from post_route(b, blk, room)
            yield from post_shared(b, room, phase)
            scr_free[:] = [l_y.done(), PE.last(), DV.last(), AC.last(), PL.last(), *all_of(l_w2), *all_of(l_cum),
                           *all_of(l_sx), *all_of(l_sh)]
            yield

        l_zb = [line(f"l_zb{i}") for i in range(NZB)]
        l_zy = line("l_zy")
        zb_free = [None] * NZB
        tb_free = [None] * NTB
        zb_tok = {}
        heads = [(b, g) for b in range(NB) for g in range(H)]

        def load_zb(n):
            b, g = heads[n]
            s = n % NZB
            src = bass.AP(ZQ.tensor, ZQ[b].offset + g * 128, [[0, 128], [H * 128, H], [1, 128]])
            zb_tok[n] = SP.dma(l_zb[s], ZB[:, s * NT:(s + 1) * NT].rearrange("p (h u) -> p h u", u=128), src,
                               zb_free[s], front[b][0])

        def zero_gen():
            for n in range(NTILE // 4):
                for c in range(1, NCH):
                    SP.dma(l_zy, Yv[c][n], view(zero[:, 0:1], 0, [[0, 4], [1, 256]]), z_ready)
                yield
                yield

        def run(gen, steps):
            for _ in range(steps):
                try:
                    next(gen)
                except StopIteration:
                    return

        def chain(*gens):
            for g in gens:
                yield from g

        ctx_tok = [None]
        tcount = [0]

        def next_tile():
            tb = tcount[0] % NTB
            tcount[0] += 1
            return tb, TB[:, tb * NT:(tb + 1) * NT]

        def quad_out(q, tb, cT, *ready):
            k = 7
            for t4 in range(4):
                for i in range(4):
                    p = PE.op(lambda e: e.transpose(ps[k][:, 128 * i:128 * i + 128],
                                                    cT[:, 512 * t4 + 128 * i:512 * t4 + 128 * i + 128],
                                                    ident[:, :]), *take(k, *ready), inc=(i == 3))
                c = DV.op(lambda e: e.tensor_tensor(
                    view(ctxn[:, 0, 0:1], 4 * t4 * C + 64 * q, [[C, 4], [16, 4], [1, 16]]),
                    view(ps[k][:, 0:1], 0, [[128, 4], [32, 4], [1, 16]]),
                    view(sB[:, 4 * q:4 * q + 1], 0, [[0, 4], [1, 4], [0, 16]]), ALU.mult),
                    p, sB_ready, ctxn_free[0])
                bank_free[k] = c
                ctx_tok[0] = c
                tb_free[tb] = p
                yield

        def attention(b, bg):
            zq, v_done, nz = front[b]
            par = b % 2
            qg = iter(())
            for q in range(4):
                base = b * H + 4 * q
                for j in range(4):
                    if base + j not in zb_tok:
                        load_zb(base + j)
                for kb in range(KB):
                    ts = []
                    for j in range(4):
                        n = base + j
                        g = 4 * q + j
                        s = n % NZB
                        tb, T = next_tile()
                        col = kb * H + g
                        a = AC.op(lambda e: e.activation(
                            T, ZB[:, s * NT:(s + 1) * NT], ACT.Abs, bias=nzk[par][:, col:col + 1], scale=1.0),
                            zb_tok[n], tb_free[tb], nz)
                        if kb == KB - 1:
                            zb_free[s] = a
                            if n + NZB < len(heads) and heads[n + NZB][0] in front:
                                load_zb(n + NZB)
                        m = DV.op(lambda e: e.tensor_scalar(T, T, bb[:, g:g + 1], bb[:, g:g + 1],
                                                            ALU.min, ALU.subtract), a, b_ready)
                        ts.append((T, m, tb))
                        run(qg, 1)
                        run(bg, 1)
                    if kb == KB - 1:
                        cb_, cT = next_tile()
                    for nn in range(4):
                        for j in range(4):
                            T, m, tb = ts[j]
                            o = kb * C + (4 * q + j) * D
                            p = PE.op(lambda e: e.matmul(
                                ps[nn][32 * j:32 * j + 32, :], V[par][:, o:o + 32],
                                T[:, 512 * nn:512 * nn + 512], start=(kb == 0), stop=(kb == KB - 1)),
                                m, v_done, bank_free[nn], inc=(j == 3))
                        if kb == KB - 1:
                            if nn % 2:
                                c = evA = AC.op(lambda e: e.activation(
                                    cT[:, 512 * nn:512 * nn + 512], ps[nn][:, :], ACT.Copy), p, tb_free[cb_])
                            else:
                                c = evD = DV.op(lambda e: e.tensor_copy(
                                    cT[:, 512 * nn:512 * nn + 512], ps[nn][:, :]), p, tb_free[cb_])
                            bank_free[nn] = c
                    for _, _, tb in ts:
                        tb_free[tb] = p
                qg = quad_out(q, cb_, cT, evA, evD)
            V_free[par] = p
            run(qg, 1000)
            run(bg, 100000)

        run(front_gen(0), 100000)
        for b in range(NB):
            gens = []
            if b:
                gens.append(post_gen(b - 1, ctx_tok[0]))
            if b + 1 < NB:
                gens.append(front_gen(b + 1))
            if b == 0:
                gens.append(zero_gen())
            attention(b, chain(*gens))

        def in_turn(gens):
            gens = list(gens)
            while gens:
                for g in list(gens):
                    try:
                        next(g)
                    except StopIteration:
                        gens.remove(g)

        room = Room(True)
        phase = [*scr_free, PE.last(), AC.last(), DV.last()]
        b = NB - 1
        in_turn([post_rows(b, blk, room, phase, ctx_tok[0]) for blk in range(4)])
        run(post_logits(b, room, phase), 100000)
        in_turn([post_route(b, blk, room) for blk in range(4)])
        shared = post_shared(b, room, phase)

        l_bs = line("l_bs")
        l_bb = line("l_bb")
        BB = ZB[:, 0:NE * NTILE]
        MB = ZB[:, NE * NTILE:2 * NE * NTILE]
        Z0 = ctxn[:, 0, 0:1]
        tau, tac, off, tok, e64, over, fi = [view(Z0, NE * i, [[1, NE]]) for i in range(7)]
        idx1 = view(Z0, NE * 7, [[1, NE]]).bitcast(i32)
        idx2 = view(Z0, NE * 8, [[1, NE]]).bitcast(i32)
        e64i = view(Z0, NE * 9, [[1, NE]]).bitcast(i32)
        t = SP.dma(l_bs, BASE.rearrange("a (e i) -> (a e) i", i=NTILE), bs[:, :], DV.last())
        t = SP.dma(l_bb, BB, bass.AP(BASE.tensor, BASE.offset, [[0, 128], [1, NE * NTILE]]), t, AC.last())
        a = PL.op(lambda e: e.iota(e64i, pattern=[[NTILE, NE]], base=0, channel_multiplier=0), ctxn_free[0],
                  DV.last())
        a = PL.op(lambda e: e.tensor_copy(e64, e64i), a)
        m = DV.op(lambda e: e.tensor_scalar(MB, BB, scol[:, 0:1], None, ALU.is_le), t, s_ready, ctxn_free[0])
        m = DV.op(lambda e: e.tensor_reduce(tau, view(MB, 0, [[NTILE, NE], [1, NTILE]]), AX.X, ALU.add), m)
        m2 = DV.op(lambda e: e.tensor_scalar(tac, tau, float(NTILE - 1), None, ALU.min), m)
        m3 = DV.op(lambda e: e.tensor_scalar(over, tau, float(NTILE) - 0.5, scol[:, 0:1], ALU.is_gt, ALU.mult))
        m4 = DV.op(lambda e: e.tensor_tensor(fi, tac, e64, ALU.add), m2, a)
        i1 = DV.op(lambda e: e.tensor_copy(idx1, fi), m4)
        m5 = DV.op(lambda e: e.tensor_scalar(tac, tac, 128.0, None, ALU.mult), m4)

        GN = 8
        G0 = V[0][:, 0:1]
        GR = [view(G0, 0, [[128, GN], [1, 128]]), view(G0, 1024, [[128, GN], [1, 128]])]
        GC = view(G0, 2048, [[128, GN], [1, 128]])
        cum_rows = CUM.rearrange("e i t -> (e i) t")
        l_g = [line("l_g0"), line("l_g1")]
        idx_ready = {}
        g_state = {"gc": [None, None], "r": None, "gt": {}}

        def gather_slots(grp):
            h = grp % 2
            for i in range(GN):
                e_ = grp * GN + i
                g_state["gt"][grp] = PL.transfer(l_g[h], lambda e: e.indirect_dma_start(
                    GR[h][:, i, :], None, cum_rows,
                    bass.IndirectOffsetOnAxis(ap=idx1[:, e_:e_ + 1].bitcast(u32), axis=0)),
                    i1, *all_of(l_cum), g_state["gc"][h])

        def find_slots(grp):
            h = grp % 2
            sl = slice(grp * GN, (grp + 1) * GN)
            gc = DV.op(lambda e: e.tensor_scalar(GC, GR[h], scol[:, 0:1], None, ALU.is_le), g_state["gt"][grp],
                       g_state["r"])
            g_state["gc"][h] = gc
            r = DV.op(lambda e: e.tensor_reduce(off[:, sl], GC, AX.X, ALU.add), gc)
            g_state["r"] = r
            r = DV.op(lambda e: e.tensor_tensor(tok[:, sl], off[:, sl], tac[:, sl], ALU.add), r, m5)
            r = DV.op(lambda e: e.tensor_tensor(fi[:, sl], tok[:, sl], over[:, sl], ALU.add), r, m3)
            idx_ready[grp] = DV.op(lambda e: e.tensor_copy(idx2[:, sl], fi[:, sl]), r)

        NX = 6
        l_ew = [line(f"l_ew{i}") for i in range(NX)]
        l_xe = [line(f"l_xe{i}") for i in range(NX)]
        l_sc = [line(f"l_sc{i}") for i in range(NCH)]
        E0 = V[1][:, 0:1]
        Z1 = ZB[:, 0:1]
        wgu = [view(Z1, 8192 + 320 * i, [[1, 256]]) for i in range(NX)]
        W1 = TB[:, 0:1]
        WX = 8192
        wgu = [view(W1, WX + 768 * i, [[256, 2], [1, 256]]) for i in range(NX)]
        wdn = [view(W1, WX + 768 * i + 512, [[1, 256]]) for i in range(NX)]
        xe = [view(W1, WX + 4608 + 320 * i, [[1, 320]]) for i in range(NX)]
        ye = [view(E0, 256 * i, [[1, 256]]) for i in range(NX)]
        xeT = [view(E0, 1536 + 256 * i, [[128, 2], [1, 128]]) for i in range(2)]
        ae = [view(E0, 2048 + 128 * i, [[1, 128]]) for i in range(2)]
        w_free, x_free, xT_free, a_free, y_free = [None] * NX, [None] * NX, [None] * 2, [None] * 2, [None] * NX
        ew, xt = {}, {}
        begun = [*all_of(l_w2), *all_of(l_cum), PE.last(), DV.last(), PL.last()]

        def load_expert(n):
            s = n % NX
            SP.dma(l_ew[s], wgu[s], egu_w[n].rearrange("(k p) f -> p k f", p=128), w_free[s], *begun)
            ew[n] = SP.dma(l_ew[s], wdn[s], edn_w[n], w_free[s])

        def gather_expert(n):
            s = n % NX
            xt[n] = PL.transfer(l_xe[s], lambda e: e.indirect_dma_start(
                xe[s], None, XH, bass.IndirectOffsetOnAxis(ap=idx2[:, n:n + 1].bitcast(u32), axis=0)),
                idx_ready[n // GN], x_free[s], *begun, *all_of(l_sh), zero_sent)

        for n in range(NX - 1):
            load_expert(n)
        gather_slots(0)
        gather_slots(1)
        run(shared, 12)
        find_slots(0)
        for n in range(NX - 1):
            gather_expert(n)
        run(shared, 12)
        find_slots(1)
        AH = 3
        sc_tok = [None] * NCH
        pend = {}

        def finish(n):
            s, c = n % NX, (n % NCH if n >= 30 else 1 + n % (NCH - 1))
            sc_tok[c] = PL.transfer(l_sc[c], lambda e: e.indirect_dma_start(
                Y[c], bass.IndirectOffsetOnAxis(ap=idx2[:, n:n + 1].bitcast(u32), axis=0), ye[s], None,
                compute_op=ALU.add), pend[n], sc_tok[c], *([l_y.done()] if c == 0 else [l_zy.done()]), zero_sent)
            y_free[s] = sc_tok[c]

        for n in range(NE):
            if n % GN == 0 and n // GN + 2 < NE // GN:
                gather_slots(n // GN + 2)
            if n % GN == GN - 4 and n // GN + 2 < NE // GN:
                find_slots(n // GN + 2)
            if n + NX - 1 < NE:
                load_expert(n + NX - 1)
                gather_expert(n + NX - 1)
            run(shared, 5)
            s, s2 = n % NX, n % 2
            k = 0 + n % 2
            for c in range(2):
                p = PE.op(lambda e: e.transpose(ps[k][:, 128 * c:128 * c + 128], xe[s][:, 128 * c:128 * c + 128],
                                                ident[:, :]), *take(k, xt[n]), inc=(c == 1))
            v = DV.op(lambda e: e.tensor_copy(xeT[s2], view(ps[k][:, 0:1], 0, [[128, 2], [1, 128]])),
                      p, xT_free[s2], *begun)
            bank_free[k] = v
            k = 2
            for f in range(2):
                for c in range(2):
                    p = PE.op(lambda e: e.matmul(
                        ps[k][:, 128 * f:128 * f + 128], wgu[s][:, c, 128 * f:128 * f + 128], xeT[s2][:, c, :],
                        start=(c == 0), stop=(c == 1)), *take(k, v, ew[n]), inc=(f == 1 and c == 1))
            xT_free[s2] = p
            a = AC.op(lambda e: e.activation(ae[s2], ps[k][:, 0:128], ACT.Silu), p, a_free[s2], *begun)
            v = DV.op(lambda e: e.tensor_tensor(ae[s2], ae[s2], ps[k][:, 128:256], ALU.mult), a)
            bank_free[k] = v
            k = 3
            p = PE.op(lambda e: e.matmul(ps[k][:, 0:256], ae[s2], wdn[s], start=True, stop=True), *take(k, v))
            a_free[s2] = w_free[s] = p
            pend[n] = AC.op(lambda e: e.activation(ye[s], ps[k][:, 0:256], ACT.Copy,
                                                   scale=xe[s][:, C + n:C + n + 1]), p, y_free[s])
            bank_free[k] = x_free[s] = pend[n]
            if n:
                finish(n - 1)
        finish(NE - 1)
        run(shared, 100000)

        NF = 3
        l_f = [line(f"l_f{i}") for i in range(NF)]
        l_o = [line(f"l_o{i}") for i in range(NF)]
        F0 = TB[:, 0:1]
        yt = [[view(F0, 5120 * i + 1024 * c, [[256, 4], [1, 256]]) for c in range(NCH + 2)] for i in range(NF)]
        endt = [PE.last(), DV.last(), AC.last(), *all_of(l_sh), *all_of(l_w2)]
        NG = NTILE // 4
        f_tok, f_rs, f_in = {}, {}, {}

        def f_load(n):
            s = n % NF
            for c in range(NCH):
                SP.dma(l_f[s], yt[s][c], Yv[c][n], *sc_tok, l_y.done(), l_zy.done(), l_o[s].done(), *endt)
            f_in[n] = SP.dma(l_f[s], yt[s][NCH], X1v[n], *all_of(l_sx))

        def f_sum(n):
            s = n % NF
            y = yt[s]
            a = PL.op(lambda e: e.tensor_tensor(y[1], y[1], y[2], ALU.add), f_in[n])
            v = DV.op(lambda e: e.tensor_tensor(y[0], y[0], y[1], ALU.add), a)
            f_rs[n] = rstd(s, lambda i: y[0][:, i, :], v)

        def f_out(n):
            s = n % NF
            y = yt[s]
            v = normalize(s, lambda i: y[0][:, i, :], lambda i: y[0][:, i, :], f_rs[n])
            v = DV.op(lambda e: e.tensor_tensor(y[0], y[0], y[NCH], ALU.add), v)
            SP.dma(l_o[s], outv[n], y[0], v)

        for n in range(NF):
            f_load(n)
        f_sum(0)
        for n in range(NG):
            if n + 1 < NG:
                f_sum(n + 1)
            f_out(n)
            if n + NF < NG:
                f_load(n + NF)
        SP.wait(*all_of(l_o), *all_of(l_sc), l_y.done(), l_zy.done(), l_zero.done(), l_bs.done(), *all_of(l_cum),
                *all_of(l_w2), *all_of(l_sh), *all_of(l_sx), l_zq.done())


_A = 'L0_attn_'
_F = 'L0_ffn_'


def kernel(**inputs):
    import numpy as _np
    import concourse.bacc as _bacc
    from concourse import mybir as _mybir
    from concourse.bass_utils import run_bass_kernel_spmd as _run

    g = lambda n: _np.asarray(inputs[n])
    lay = {
        "x": g(_A + 'hidden_states'),
        "WqT": g(_A + 'Wq').T, "bq": g(_A + 'bq').reshape(2, 128).T,
        "WkT": g(_A + 'Wk').T, "bk": g(_A + 'bk').reshape(2, 128).T,
        "WvT": g(_A + 'Wv').T, "bv": g(_A + 'bv'),
        "WpT": g(_A + 'Wproj').reshape(16, 16, 16).transpose(2, 1, 0),
        "lbw": g(_A + 'log_bandwidth'),
        "gates_w": _np.concatenate([g(_F + 'gate_w'), g(_F + 'shared_gate_w')], axis=1),
        "sgu_w": g(_F + 'shared_gate_up_w'), "sdn_w": g(_F + 'shared_down_w'),
        "egu_w": g(_F + 'expert_gate_up_w'), "edn_w": g(_F + 'expert_down_w'),
    }
    nc = _bacc.Bacc("TRN2", target_bir_lowering=False, num_devices=1)
    arrays, args = {}, []
    for n, a in lay.items():
        a = _np.ascontiguousarray(a)
        arrays["in_" + n] = a
        args.append(nc.dram_tensor("in_" + n, a.shape, _mybir.dt.from_np(a.dtype), kind="ExternalInput").ap())
    out = nc.dram_tensor("out_0", (4, 2048, 256), _mybir.dt.float32, kind="ExternalOutput").ap()
    build(nc, *args, out)
    r = _run(nc, [arrays], core_ids=[0])
    return r.results[0]["out_0"]
```

```python
import concourse.bass as bass
from concourse import mybir
from contextlib import ExitStack

fp32 = mybir.dt.float32
u32 = mybir.dt.uint32
i32 = mybir.dt.int32
ALU = mybir.AluOpType
ACT = mybir.ActivationFunctionType
AX = mybir.AxisListType

NB, NT, C, H, D = 4, 2048, 256, 16, 16
KB = NT // 128
NE, CAP, TOPK = 64, 128, 8
NI, NS = 128, 512
TOK = NB * NT
NTILE = TOK // 128
NZB = 5
NCH = 2
NTB = 8
RATE = [0.4, 1.0, 1.0, 0.7]
SHN = 3
VW = KB * C + 16


class Stream:

    def __init__(self, eng, sem):
        self.eng, self.sem, self.n, self.reached = eng, sem, 0, {}

    def wait(self, *after):
        for t in after:
            if t is not None and t[1] > self.reached.get(id(t[0]), 0):
                self.eng.wait_ge(t[0], t[1])
                self.reached[id(t[0])] = t[1]

    def op(self, fn, *after, inc=True):
        self.wait(*after)
        ins = fn(self.eng)
        if inc:
            ins.then_inc(self.sem, 1)
            self.n += 1
        return (self.sem, self.n)

    def transfer(self, line, fn, *after):
        self.wait(*after)
        fn(self.eng).then_inc(line.sem, 16)
        line.n += 16
        return (line.sem, line.n)

    def dma(self, line, out, in_, *after):
        return self.transfer(line, lambda e: e.dma_start(out, in_), *after)

    def last(self):
        return (self.sem, self.n)


class Line:

    def __init__(self, sem):
        self.sem, self.n = sem, 0

    def done(self):
        return (self.sem, self.n) if self.n else None


def view(a, offset, dims):
    return bass.AP(a.tensor, a.offset + offset, [list(a.ap[0])] + [list(d) for d in dims])


def build(nc, x, WqT, bq, WkT, bk, WvT, bv, WpT, lbw, gates_w, sgu_w, sdn_w, egu_w, edn_w, out):
    with ExitStack() as ctx:
        def sb(name, shape, dt=fp32):
            return ctx.enter_context(nc.sbuf_tensor(name, shape, dt))

        def dram(name, shape):
            return nc.dram_tensor(name, shape, fp32, kind="Internal").ap()

        def line(name):
            return Line(ctx.enter_context(nc.semaphore(name)))

        PE = Stream(nc.tensor, ctx.enter_context(nc.semaphore("s_pe")))
        AC = Stream(nc.scalar, ctx.enter_context(nc.semaphore("s_act")))
        DV = Stream(nc.vector, ctx.enter_context(nc.semaphore("s_dve")))
        PL = Stream(nc.gpsimd, ctx.enter_context(nc.semaphore("s_pool")))
        SP = Stream(nc.sync, ctx.enter_context(nc.semaphore("s_sp")))

        ZQ = dram("zq_rows", (NB, H, H, 128))
        XH = dram("h_rows", (TOK + 128, C + NE))
        X1 = dram("x1_rows", (TOK, C))
        Y = [dram(f"y_rows{i}", (TOK + 128, C)) for i in range(NCH)]
        CUM = dram("cum_rows", (NE, NTILE, 128))

        TB = sb("TB", [128, NTB * NT])
        ZB = sb("ZB", [128, NZB * NT])
        V = [sb(f"V{i}", [128, VW]) for i in range(2)]
        ctxn = sb("ctxn", [128, KB, C])
        scr = sb("scr", [128, 4096])
        BD = sb("BD", [128, 16, 128])
        wq_sb = sb("wq_sb", [128, 2, C])
        wk_sb = sb("wk_sb", [128, 2, C])
        wv_sb = sb("wv_sb", [128, 2, C])
        wg_sb = sb("wg_sb", [128, 2, NE + 1])
        wsgu = sb("wsgu", [128, 2, 2 * NS])
        wsdn = sb("wsdn", [128, 4, C])
        bqc = sb("bqc", [128, 2])
        bkc = sb("bkc", [128, 2])
        bvb = sb("bvb", [128, C])
        ident = sb("ident", [128, 128])
        bb = sb("bb", [128, H])
        bt = sb("bt", [128, 3, H])
        sB = sb("sB", [128, H])
        nzk = [sb(f"nzk{i}", [128, C]) for i in range(2)]
        mhalf = sb("mhalf", [128, 4])
        st6 = [sb(f"st6{i}", [128, 4, 6]) for i in range(5)]
        mv = [sb(f"mv{i}", [128, 4, 2]) for i in range(5)]
        ve = [sb(f"ve{i}", [128, 4]) for i in range(5)]
        rs = [sb(f"rs{i}", [128, 4]) for i in range(5)]
        zero = sb("zero", [128, 320])
        Lg = sb("Lg", [128, KB, NE + 1])
        sg = sb("sg", [128, KB])
        carry = sb("carry", [NE, 1])

        scol = sb("scol", [128, 1])
        scoli = sb("scoli", [128, 1], i32)

        ps = [ctx.enter_context(nc.psum_tensor(f"ps{i}", [128, 512], fp32)) for i in range(8)]
        bank_free = [None] * 8

        xT_v = x.rearrange("b (k i p) c -> b k p i c", p=128, i=4)
        X1v = X1.rearrange("(n i p) c -> n p i c", p=128, i=4)
        XHv = XH[0:TOK, :].rearrange("(n i p) c -> n p i c", p=128, i=4)
        Yv = [y_[0:TOK, :].rearrange("(n i p) c -> n p i c", p=128, i=4) for y_ in Y]
        outv = out.rearrange("b (k i p) c -> (b k) p i c", p=128, i=4)

        l_w = line("l_w")
        l_x = [line(f"l_x{i}") for i in range(4)]
        for i in range(4):
            SP.dma(l_x[i], ctxn[:, 4 * i:4 * i + 4, :], xT_v[0, i])
        l_zero = line("l_zero")
        l_sgu = line("l_sgu")
        for dst, src in ((wq_sb, WqT), (wk_sb, WkT), (wv_sb, WvT)):
            AC.dma(l_w, dst[:, :, :], src.rearrange("(k p) n -> p k n", p=128))
        for dst, src in ((bqc, bq), (bkc, bk)):
            AC.dma(l_w, dst[:, :], src)
        AC.dma(l_w, bvb[:, :], bass.AP(bv.tensor, bv.offset, [[0, 128], [1, C]]))
        AC.dma(l_w, bb[:, :], bass.AP(lbw.tensor, lbw.offset, [[0, 128], [1, H]]))
        bd0 = PL.op(lambda e: e.memset(BD[:, :, :], 0.0))
        w_ready = None
        for h in range(8):
            w_ready = (SP if h % 2 else AC).dma(l_w, BD[16 * h:16 * h + 16, :, 16 * h:16 * h + 16], WpT, bd0)
        SP.dma(l_sgu, wg_sb[:, :, :], gates_w.rearrange("(k p) n -> p k n", p=128))
        SP.dma(l_sgu, wsgu[:, :, :], sgu_w.rearrange("(k p) n -> p k n", p=128))
        wf_ready = SP.dma(l_sgu, wsdn[:, :, :], sdn_w.rearrange("(k p) n -> p k n", p=128))

        i0 = PL.op(lambda e: e.memset(ident[:, :], 0.0))
        id_ready = PL.op(lambda e: e.affine_select(out=ident[:, :], in_=ident[:, :], compare_op=ALU.not_equal,
                                                   fill=1.0, base=0, pattern=[[-1, 128]], channel_multiplier=1), i0)
        mh_ready = PL.op(lambda e: e.memset(mhalf[:, :], -0.5))
        io = PL.op(lambda e: e.iota(scoli[:, :], pattern=[[0, 1]], base=0, channel_multiplier=1))
        s_ready = PL.op(lambda e: e.tensor_copy(scol[:, :], scoli[:, :]), io)
        carry_tok = [DV.op(lambda e: e.memset(carry[:, :], 0.0))]
        for i in range(2):
            v_pad = DV.op(lambda e, i=i: e.memset(V[i][:, KB * C:VW], 0.0))
        z_ready = DV.op(lambda e: e.memset(zero[:, :], 0.0))
        SP.dma(l_zero, XH[TOK:TOK + 128, :], zero[:, 0:C + NE], z_ready)
        zero_sent = SP.dma(l_zero, Y[0][TOK:TOK + 128, :], zero[:, 0:C])

        t = AC.op(lambda e: e.activation(bt[:, 0, :], bb[:, :], ACT.Abs), w_ready)
        t = AC.op(lambda e: e.activation(bt[:, 1, :], bt[:, 0, :], ACT.Exp, scale=-1.0), t)
        t = AC.op(lambda e: e.activation(bt[:, 2, :], bt[:, 1, :], ACT.Ln, bias=1.0), t)
        t1 = DV.op(lambda e: e.tensor_scalar(bt[:, 0, :], bb[:, :], 0.0, None, ALU.max), t)
        t2 = DV.op(lambda e: e.tensor_tensor(bt[:, 1, :], bt[:, 0, :], bt[:, 2, :], ALU.add), t1)
        b_ready = DV.op(lambda e: e.tensor_scalar(bb[:, :], bt[:, 1, :], 1e-4, None, ALU.add), t2)
        t3 = DV.op(lambda e: e.tensor_scalar(bt[:, 0, :], bb[:, :], -float(NT), None, ALU.mult), b_ready)
        sB_ready = DV.op(lambda e: e.reciprocal(sB[:, :], bt[:, 0, :]), t3)

        def take(bank, *after):
            return [bank_free[bank], *after]

        free_banks = [0, 1, 2, 3, 4, 5, 6]

        credit = [1e9]

        def unit(fill, evac, delay=3, ready=None, cost=2):
            while not free_banks or credit[0] <= 0 or (ready and not ready()):
                yield
            credit[0] -= cost
            k = free_banks.pop(0)
            p = fill(k)
            for _ in range(delay):
                yield
            bank_free[k] = evac(k, p)
            free_banks.append(k)

        def together(*gens):
            live = list(gens)
            while True:
                for g in list(live):
                    try:
                        next(g)
                    except StopIteration:
                        live.remove(g)
                if not live:
                    return
                yield

        ln_free = [None] * 5

        def rstd(s, ap4, *after):
            for i in range(4):
                a = DV.op(lambda e: e.bn_stats(st6[s][:, i, :], ap4(i)), *after, ln_free[s], inc=(i == 3))
            for i in range(4):
                m = DV.op(lambda e: e.bn_aggr(mv[s][:, i, :], st6[s][:, i, :]), a, inc=(i == 3))
            p = PL.op(lambda e: e.tensor_scalar(ve[s][:, :], view(mv[s][:, 0, 1:2], 0, [[2, 4]]), 1e-5, None,
                                                ALU.add), m)
            return PL.op(lambda e: e.tensor_tensor(rs[s][:, :], ve[s][:, :], mhalf[:, 0:4], ALU.pow), p, mh_ready)

        def normalize(s, dst4, src4, *ready):
            for i in range(4):
                n = DV.op(lambda e: e.tensor_scalar(dst4(i), src4(i), mv[s][:, i, 0:1], rs[s][:, i:i + 1],
                                                    ALU.subtract, ALU.mult), *ready, inc=(i == 3))
            ln_free[s] = n
            return n

        def move(on_dve, dst, src, *after):
            if on_dve:
                return DV.op(lambda e: e.tensor_copy(dst, src), *after)
            return AC.op(lambda e: e.activation(dst, src, ACT.Copy), *after)

        def flip(k, c, src4, *ready):
            for i in range(4):
                p = PE.op(lambda e: e.transpose(ps[k][:, 128 * i:128 * i + 128],
                                                src4(i)[:, 128 * c:128 * c + 128], ident[:, :]),
                          *take(k, *ready, id_ready), inc=(i == 3))
            return p

        l_zq = line("l_zq")
        front = {}
        mixed_tok = {}
        scr_free = [zero_sent]
        V_free = [None, None]

        def front_gen(b):
            par = b % 2
            T0 = TB[:, 0:1]
            S0 = scr[:, 0:1]
            if b:
                xg = [view(S0, 0, [[256, 4], [1, 256]])] * 4
                hT = [view(S0, 1024, [[512, 2], [1, 512]])] * 4
                QK = [view(S0, 2048, [[512, 4], [1, 512]])] * 4
            else:
                xg = [ctxn[:, 4 * i:4 * i + 4, :] for i in range(4)]
                hT = [view(S0, 1024 * i, [[512, 2], [1, 512]]) for i in range(4)]
                QK = [view(T0, 8192 + 2048 * i, [[512, 4], [1, 512]]) for i in range(4)]
            Zs = view(Lg[:, 0, 0:1], 0, [[128, 4], [1, 128]])
            phase = list(scr_free)
            st = {"hT": {}, "hT_free": [], "qk": {}, "qk_free": []}
            fetched, used, mixed = [0], [0] * 4, [0]

            def fetch(blk, *after):
                SP.dma(l_x[blk], xg[blk], xT_v[b, blk], *phase, *after)
                fetched[0] = blk + 1

            def turned(blk, c):
                def fill(k):
                    p = flip(k, c, lambda i: xg[blk][:, i, :], st["n", blk])
                    if b and c == 1 and blk < 3:
                        fetch(blk + 1, p)
                    return p

                def evac(k, p):
                    st["hT"][blk, c] = move(b or c == 0, hT[blk][:, c, :], ps[k][:, :], p, *st["hT_free"], *phase)
                    return st["hT"][blk, c]
                return unit(fill, evac, ready=lambda: not b or not blk or used[blk - 1] == 6, cost=0.5)

            def products(k, blk, todo):
                for out_, lhs, rhs, c, last in todo:
                    p = PE.op(lambda e: e.matmul(out_, lhs, rhs, start=(c == 0), stop=(c == 1)),
                              *take(k, st["hT"][blk, 0], st["hT"][blk, 1], w_ready), inc=last)
                if b:
                    st["hT_free"] = [p]
                used[blk] += 1
                return p

            def values(blk, pair):
                def fill(k):
                    return products(k, blk, [
                        (ps[k][:, 256 * i:256 * i + 256],
                         hT[blk][:, c, 256 * pair + 128 * i:256 * pair + 128 * i + 128], wv_sb[:, c, :], c,
                         i == 1 and c == 1) for i in range(2) for c in range(2)])

                def evac(k, p):
                    o = (4 * blk + 2 * pair) * C
                    st["v"] = DV.op(lambda e: e.tensor_tensor(
                        view(V[par][:, o:o + 1], 0, [[256, 2], [1, 256]]),
                        view(ps[k][:, 0:1], 0, [[256, 2], [1, 256]]),
                        view(bvb[:, 0:1], 0, [[0, 2], [1, 256]]), ALU.add), p, V_free[par], v_pad)
                    return st["v"]
                return unit(fill, evac)

            def project(blk, j):
                (w, bias), m = ((wq_sb, bqc), (wk_sb, bkc))[j // 2], j % 2

                def fill(k):
                    return products(k, blk, [(ps[k][:, :], w[:, c, 128 * m:128 * m + 128], hT[blk][:, c, :], c,
                                              c == 1) for c in range(2)])

                def evac(k, p):
                    dst = QK[blk][:, j, :]
                    after = (p, *st["qk_free"], *phase)
                    if b or j % 2:
                        q = DV.op(lambda e: e.tensor_scalar(dst, ps[k][:, :], bias[:, m:m + 1], None, ALU.add),
                                  *after)
                    else:
                        q = AC.op(lambda e: e.activation(dst, ps[k][:, :], ACT.Identity, bias=bias[:, m:m + 1]),
                                  *after)
                    st["qk"][blk, j] = q
                    return q
                return unit(fill, evac, ready=lambda: not b or mixed[0] == blk)

            def mix(blk):
                def fill(k):
                    for tt in range(16):
                        p = PE.op(lambda e: e.matmul(
                            ps[k][:, 0:128], BD[:, tt, :], view(QK[blk][:, 0, 0:1], tt, [[512, 4], [16, 32]]),
                            start=(tt == 0), stop=(tt == 15)),
                            *take(k, *[st["qk"][blk, j] for j in range(4)], w_ready), inc=(tt == 15))
                    if b:
                        st["qk_free"] = [p]
                    mixed[0] += 1
                    mixed_tok[blk] = p
                    return p

                def evac(k, p):
                    st["z"] = DV.op(lambda e: e.tensor_copy(
                        Zs[:, :, 32 * blk:32 * blk + 32], view(ps[k][:, 0:1], 0, [[32, 4], [1, 32]])), p, *phase)
                    return st["z"]
                return unit(fill, evac, cost=4)

            def block(blk):
                while fetched[0] <= blk:
                    yield
                if b:
                    yield
                    yield
                    yield
                xa = xg[blk]
                r = rstd(blk, lambda i: xa[:, i, :], l_x[blk].done())
                yield
                yield
                st["n", blk] = normalize(blk, lambda i: xa[:, i, :], lambda i: xa[:, i, :], r)
                yield
                yield from together(turned(blk, 0), turned(blk, 1))
                if b:
                    yield from together(values(blk, 0), values(blk, 1), *[project(blk, j) for j in range(4)])
                else:
                    yield from together(*[project(blk, j) for j in range(4)])
                yield from mix(blk)

            if b:
                fetch(0)
            else:
                fetched[0] = 4
            yield from together(*[block(i) for i in range(4)])
            zq = None
            for m in range(2):
                dst = bass.AP(ZQ.tensor, ZQ[b].offset + m * 8 * H * 128, [[128, 128], [1, 128]])
                zq = SP.dma(l_zq, dst, Zs[:, m, :], st["z"])

            def fill(k):
                for m in range(2):
                    p = PE.op(lambda e: e.transpose(ps[k][:, 128 * m:128 * m + 128], Zs[:, 2 + m, :],
                                                    ident[:, :]), *take(k, st["z"]), inc=(m == 1))
                return p

            def evac(k, p):
                st["nz"] = DV.op(lambda e: e.tensor_scalar(nzk[par][:, :], ps[k][:, 0:256], -1.0, None, ALU.mult),
                                 p, V_free[par])
                return st["nz"]
            yield from unit(fill, evac, cost=0.5)
            if not b:
                yield from together(*[values(blk, i) for blk in range(4) for i in range(2)])
            scr_free[:] = [PE.last(), DV.last(), AC.last(), zq]
            front[b] = (zq, st["v"], st["nz"])
            yield

        l_a = [line(f"l_a{i}") for i in range(4)]
        l_h = line("l_h")
        l_sx = [line(f"l_sx{i}") for i in range(4)]
        l_sh = [line(f"l_sh{i}") for i in range(4)]
        l_w2 = [line(f"l_w2{i}") for i in range(4)]
        l_y = line("l_y")
        l_cum = [line(f"l_cum{i}") for i in range(4)]
        ctxn_free = [None]

        def all_of(lines):
            return [l.done() for l in lines]

        class Room:

            def __init__(self, tail):
                T0 = TB[:, 0:1]
                S0 = scr[:, 0:1]
                if tail:
                    self.x = [view(T0, 1024 * i, [[256, 4], [1, 256]]) for i in range(4)]
                    self.h = [view(T0, 4096 + 1024 * i, [[256, 4], [1, 256]]) for i in range(4)]
                    self.r = [(T0, 8192 + 1344 * i) for i in range(4)]
                    self.hT = [view(S0, 1024 * i, [[512, 2], [1, 512]]) for i in range(4)]
                    self.act = view(T0, 0, [[512, 4], [1, 512]])
                    self.y = view(T0, 2048, [[256, 4], [1, 256]])
                else:
                    self.x = [view(S0, 3072, [[256, 4], [1, 256]])] * 4
                    self.h = [view(S0, 0, [[256, 4], [1, 256]])] * 4
                    self.r = [(S0, 1024 + 1344 * (i % 2)) for i in range(4)]
                    self.hT = [view(S0, 1024, [[512, 2], [1, 512]])] * 4
                    self.act = view(S0, 2048, [[512, 4], [1, 512]])
                    self.y = self.h[0]
                self.tail = tail
                self.x_free, self.h_free, self.r_free = [[None] * 4 for _ in range(3)]
                self.h_tok = [None] * 4
                self.hT_tok = {}
                self.hT_free = [None]
                self.flipped = self.routed = self.gated = 0
                self.lg = self.sg = None

        def post_rows(b, blk, room, phase, ctx_ready):
            xg, hg = room.x[blk], room.h[blk]
            prev = (blk - 1) % 4
            same = [] if room.tail else [l_sx[prev].done(), room.x_free[prev]]
            ld = SP.dma(l_a[blk], xg, xT_v[b, blk], *phase, *same)
            cx = lambda i: ctxn[:, 4 * blk + i, :]
            r = rstd(blk, cx, ctx_ready)
            yield
            yield
            n = normalize(blk, cx, cx, r)
            yield
            add = lambda e: e.tensor_tensor(xg, xg, ctxn[:, 4 * blk:4 * blk + 4, :], ALU.add)
            xs = (DV if room.tail else PL).op(add, ld, n)
            ctxn_free[0] = xs
            yield
            yield
            SP.dma(l_sx[blk], X1v[4 * b + blk], xg, xs)
            r = rstd(blk, lambda i: xg[:, i, :], xs)
            yield
            yield
            while not room.tail and room.flipped < 2 * blk:
                yield
            n = normalize(blk, lambda i: hg[:, i, :], lambda i: xg[:, i, :], r, *phase,
                          *([] if room.tail else [l_sh[prev].done(), room.h_free[0]]))
            room.x_free[blk] = room.h_tok[blk] = n
            SP.dma(l_sh[blk], XHv[4 * b + blk][:, :, 0:C], hg, n)
            yield

        def turn_h(blk, c, room, phase, ready):
            def fill(k):
                p = flip(k, c, lambda i: room.h[blk][:, i, :], ready)
                room.h_free[0] = p
                room.flipped += 1
                return p

            def evac(k, p):
                room.hT_tok[blk, c] = move(c == 0, room.hT[blk][:, c, :], ps[k][:, :], p,
                                           *room.hT_free, *phase)
                return room.hT_tok[blk, c]
            return unit(fill, evac, cost=0.5)

        def post_logits(blk, room, phase):
            yield from together(*[turn_h(blk, c, room, phase, room.h_tok[blk]) for c in range(2)])

            def fill(k):
                for i in range(4):
                    for c in range(2):
                        p = PE.op(lambda e: e.matmul(
                            ps[k][:, 65 * i:65 * i + 65], room.hT[blk][:, c, 128 * i:128 * i + 128], wg_sb[:, c, :],
                            start=(c == 0), stop=(c == 1)),
                            *take(k, room.hT_tok[blk, 0], room.hT_tok[blk, 1], wf_ready),
                            inc=(i == 3 and c == 1))
                room.hT_free = [p]
                return p

            def evac(k, p):
                room.lg = DV.op(lambda e: e.tensor_copy(
                    Lg[:, 4 * blk:4 * blk + 4, :], view(ps[k][:, 0:1], 0, [[65, 4], [1, 65]])), p, *phase)
                return room.lg
            yield from unit(fill, evac)

        def post_route(b, blk, room, phase):
            base, o = room.r[blk]
            R4 = view(base, o, [[64, 4], [1, 64]])
            M4 = view(base, o + 256, [[64, 4], [1, 64]])
            E4 = view(base, o + 512, [[65, 4], [1, 65]])
            W4 = R4
            mx = view(base, o + 772, [[8, 4], [1, 8]])
            sm = view(base, o + 804, [[1, 4]])
            sg4 = view(base, o + 808, [[1, 4]])
            b64 = scr[0:NE, 0:1] if not room.tail else TB[0:NE, 0:1]
            cm = view(b64, o + 812, [[1, 512]])
            L4 = Lg[:, 4 * blk:4 * blk + 4, 0:NE]
            prev = (blk - 2) % 4
            free = [*phase] if room.tail else [*phase, room.r_free[prev], l_w2[prev].done(), l_cum[prev].done()]
            for i in range(4):
                a = DV.op(lambda e: e.max(mx[:, i, :], Lg[:, 4 * blk + i, 0:NE]), room.lg, *free, inc=(i == 3))
            yield
            for i in range(4):
                a2 = DV.op(lambda e: e.match_replace(
                    out=R4[:, i, :], in_to_replace=mx[:, i, :], in_values=Lg[:, 4 * blk + i, 0:NE],
                    imm_value=-3.0e38), a, inc=(i == 3))
            yield
            d = DV.op(lambda e: e.tensor_tensor(E4[:, :, 0:64], L4, view(mx, 0, [[8, 4], [0, 64]]), ALU.subtract), a)
            d = DV.op(lambda e: e.tensor_scalar(E4[:, :, 64:65], Lg[:, 4 * blk:4 * blk + 4, 64:65],
                                                -1.0, None, ALU.mult))
            mk = DV.op(lambda e: e.tensor_tensor(M4, R4, L4, ALU.not_equal), a2)
            yield
            ex = AC.op(lambda e: e.activation(E4, E4, ACT.Exp), d)

            def fill(k):
                for i in range(4):
                    pt = PE.op(lambda e: e.transpose(ps[k][0:NE, 128 * i:128 * i + 128], M4[:, i, :], ident[:, :]),
                               *take(k, mk), inc=(i == 3))
                return pt

            def evac(k, pt):
                sc = DV.op(lambda e: e.tensor_tensor_scan(
                    cm, ps[k][0:NE, :], view(zero[0:NE, 0:1], 0, [[0, 512]]), carry[:, :],
                    ALU.add, ALU.add), pt, z_ready, carry_tok[0])
                carry_tok[0] = DV.op(lambda e: e.tensor_copy(carry[:, :], cm[:, 511:512]), sc)
                SP.dma(l_cum[blk], CUM[:, 16 * b + 4 * blk:16 * b + 4 * blk + 4, :].rearrange("e i t -> e (i t)"),
                       cm, sc)
                return sc
            yield from unit(fill, evac, ready=lambda: room.routed == blk, cost=0.5)
            room.routed = blk + 1
            yield
            a = PL.op(lambda e: e.tensor_tensor(W4, E4[:, :, 0:64], M4, ALU.mult), ex, mk)
            yield
            a = DV.op(lambda e: e.tensor_reduce(sm, W4, AX.X, ALU.add), a)
            a = DV.op(lambda e: e.reciprocal(sm, sm), a)
            g = DV.op(lambda e: e.tensor_scalar(sg4, E4[:, :, 64], 1.0, None, ALU.add))
            room.sg = DV.op(lambda e: e.reciprocal(sg[:, 4 * blk:4 * blk + 4], sg4), g)
            yield
            wn = PL.op(lambda e: e.tensor_tensor(W4, W4, view(sm, 0, [[1, 4], [0, 64]]), ALU.mult), a)
            SP.dma(l_w2[blk], XHv[4 * b + blk][:, :, C:C + NE], W4, wn)
            room.r_free[blk] = room.sg
            room.gated += 1
            yield

        def post_shared(b, room, phase):
            act = room.act
            st = {"act_free": None, "s1": {}, "down": []}

            def fetch_h(blk):
                return SP.dma(l_h, room.h[blk], XHv[4 * b + blk][:, :, 0:C], *all_of(l_sh), l_y.done(),
                              room.h_free[0])

            def gate_up(blk, m, up):
                o = NS * up + 128 * m

                def fill(k):
                    for c in range(2):
                        p = PE.op(lambda e: e.matmul(
                            ps[k][:, :], wsgu[:, c, o:o + 128], room.hT[blk][:, c, :], start=(c == 0), stop=(c == 1)),
                            *take(k, room.hT_tok[blk, 0], room.hT_tok[blk, 1], wf_ready), inc=(c == 1))
                    room.hT_free = [p]
                    return p

                def evac(k, p):
                    if up:
                        st["s2"] = DV.op(lambda e: e.tensor_tensor(act[:, m, :], act[:, m, :], ps[k][:, :], ALU.mult),
                                         p, st["s1"][blk, m])
                        return st["s2"]
                    st["s1"][blk, m] = AC.op(lambda e: e.activation(act[:, m, :], ps[k][:, :], ACT.Silu), p,
                                             st["act_free"], *phase)
                    return st["s1"][blk, m]
                return unit(fill, evac, 4 if up else 3)

            def down(blk, pair):
                def fill(k):
                    for i in range(2):
                        ti = 2 * pair + i
                        for m in range(4):
                            p = PE.op(lambda e: e.matmul(
                                ps[k][:, 256 * i:256 * i + 256], act[:, m, 128 * ti:128 * ti + 128],
                                wsdn[:, m, :], start=(m == 0), stop=(m == 3)), *take(k, st["s2"]),
                                inc=(i == 1 and m == 3))
                    st["act_free"] = p
                    return p

                def evac(k, p):
                    for i in range(2):
                        ti = 2 * pair + i
                        ya = DV.op(lambda e: e.tensor_scalar(
                            room.y[:, ti, :], ps[k][:, 256 * i:256 * i + 256],
                            sg[:, 4 * blk + ti:4 * blk + ti + 1], None, ALU.mult), p, room.sg,
                            l_y.done(), l_h.done(), room.h_free[0], *phase, inc=(i == 1))
                    if pair:
                        SP.dma(l_y, Yv[0][4 * b + blk], room.y, ya)
                    return ya
                return unit(fill, evac, cost=4, ready=lambda: room.gated == 4)

            if not room.tail:
                h_ready = fetch_h(0)
                for _ in range(3):
                    yield
            for blk in range(4):
                turn = [] if room.tail else [turn_h(blk, c, room, phase, h_ready) for c in range(2)]
                yield from together(*turn, *st["down"])
                if not room.tail and blk < 3:
                    h_ready = fetch_h(blk + 1)
                yield from together(*[gate_up(blk, m, up) for m in range(4) for up in range(2)])
                st["down"] = [down(blk, 0), down(blk, 1)]
            yield from together(*st["down"])

        def post_gen(b):
            for _ in range(5):
                yield
            ctx_ready = ctx_tok[0]
            room = Room(False)
            phase = list(scr_free)
            yield from post_rows(b, 0, room, phase, ctx_ready)
            for blk in range(1, 4):
                yield from together(post_logits(blk - 1, room, phase), post_rows(b, blk, room, phase, ctx_ready))
            yield from post_logits(3, room, phase)
            phase = [*phase, *all_of(l_sx), room.x_free[3], PE.last(), DV.last()]
            yield from together(post_route(b, 0, room, phase), post_route(b, 1, room, phase))
            yield from together(post_route(b, 2, room, phase), post_route(b, 3, room, phase))
            phase = [*phase, *all_of(l_w2), *all_of(l_cum), DV.last(), PL.last()]
            yield from post_shared(b, room, phase)
            scr_free[:] = [l_y.done(), PE.last(), DV.last(), AC.last(), PL.last(), *all_of(l_w2), *all_of(l_cum),
                           *all_of(l_sx), *all_of(l_sh)]
            yield

        l_zb = [line(f"l_zb{i}") for i in range(NZB)]
        l_zy = line("l_zy")
        zb_free = [None] * NZB
        tb_free = [None] * NTB
        zb_tok = {}
        heads = [(b, g) for b in range(NB) for g in range(H)]

        def load_zb(n):
            b, g = heads[n]
            s = n % NZB
            src = bass.AP(ZQ.tensor, ZQ[b].offset + g * 128, [[0, 128], [H * 128, H], [1, 128]])
            zb_tok[n] = SP.dma(l_zb[s], ZB[:, s * NT:(s + 1) * NT].rearrange("p (h u) -> p h u", u=128), src,
                               zb_free[s], front[b][0])

        def zero_gen():
            for n in range(NTILE // 4):
                for c in range(1, NCH):
                    SP.dma(l_zy, Yv[c][n], view(zero[:, 0:1], 0, [[0, 4], [1, 256]]), z_ready)
                yield
                yield

        def run(gen, steps):
            for _ in range(steps):
                try:
                    next(gen)
                except StopIteration:
                    return

        def chain(*gens):
            for g in gens:
                yield from g

        ctx_tok = [None]
        tcount = [0]

        def next_tile():
            tb = tcount[0] % NTB
            tcount[0] += 1
            return tb, TB[:, tb * NT:(tb + 1) * NT]

        def quad_out(q, tb, cT, products):
            def scaled(t4, p):
                bank_free[7] = ctx_tok[0] = DV.op(lambda e: e.tensor_tensor(
                    view(ctxn[:, 0, 0:1], 4 * t4 * C + 64 * q, [[C, 4], [16, 4], [1, 16]]),
                    view(ps[7][:, 0:1], 0, [[128, 4], [32, 4], [1, 16]]),
                    view(sB[:, 4 * q:4 * q + 1], 0, [[0, 4], [1, 4], [0, 16]]), ALU.mult),
                    p, sB_ready, ctxn_free[0])

            for t4 in range(4):
                c = bank_free[t4] = DV.op(lambda e: e.tensor_copy(cT[:, 512 * t4:512 * t4 + 512], ps[t4][:, :]),
                                          products[t4], tb_free[tb])
                if t4:
                    scaled(t4 - 1, p)
                for i in range(4):
                    p = PE.op(lambda e: e.transpose(ps[7][:, 128 * i:128 * i + 128],
                                                    cT[:, 512 * t4 + 128 * i:512 * t4 + 128 * i + 128],
                                                    ident[:, :]), *take(7, c), inc=(i == 3))
                yield
            tb_free[tb] = p
            scaled(3, p)

        qg = iter(())

        def attention(b, bg):
            nonlocal qg
            zq, v_done, nz = front[b]
            par = b % 2
            products = [None] * 4
            credit[0] = 0
            for q in range(4):
                base = b * H + 4 * q
                for j in range(4):
                    if base + j not in zb_tok:
                        load_zb(base + j)
                for kb in range(KB):
                    ts = []
                    for j in range(4):
                        n = base + j
                        g = 4 * q + j
                        s = n % NZB
                        tb, T = next_tile()
                        col = kb * H + g
                        a = AC.op(lambda e: e.activation(
                            T, ZB[:, s * NT:(s + 1) * NT], ACT.Abs, bias=nzk[par][:, col:col + 1], scale=1.0),
                            zb_tok[n], tb_free[tb], nz)
                        if kb == KB - 1:
                            zb_free[s] = a
                            if n + NZB < len(heads) and heads[n + NZB][0] in front:
                                load_zb(n + NZB)
                        run(qg, 1)
                        credit[0] = min(credit[0] + RATE[b], 4)
                        run(bg, 1)
                        if base + 4 < len(heads) and heads[base + 4][0] in front and base + 4 not in zb_tok:
                            load_zb(base + 4)
                        m = DV.op(lambda e: e.tensor_scalar(T, T, bb[:, g:g + 1], bb[:, g:g + 1],
                                                            ALU.min, ALU.subtract), a, b_ready)
                        ts.append((T, m, tb))
                    if kb == KB - 1:
                        cb_, cT = next_tile()
                    for nn in range(4):
                        for j in range(4):
                            T, m, tb = ts[j]
                            o = kb * C + (4 * q + j) * D
                            p = PE.op(lambda e: e.matmul(
                                ps[nn][32 * j:32 * j + 32, :], V[par][:, o:o + 32],
                                T[:, 512 * nn:512 * nn + 512], start=(kb == 0), stop=(kb == KB - 1)),
                                m, v_done, bank_free[nn], inc=(j == 3))
                        products[nn] = p
                    for _, _, tb in ts:
                        tb_free[tb] = p
                qg = quad_out(q, cb_, cT, list(products))
            V_free[par] = p
            credit[0] = 1e9
            run(bg, 100000)

        run(front_gen(0), 100000)
        free_banks[:] = [4, 5, 6]
        for i in range(4):
            tb_free[4 + i] = mixed_tok[i]
        for b in range(NB):
            gens = []
            if b:
                gens.append(post_gen(b - 1))
            if b + 1 < NB:
                gens.append(front_gen(b + 1))
            if b == 0:
                gens.append(zero_gen())
            attention(b, chain(*gens))

        run(qg, 1000)
        room = Room(True)
        phase = [*scr_free, PE.last(), AC.last(), DV.last()]
        b = NB - 1
        at_end = [PE.last(), AC.last(), DV.last()]
        free_banks[:] = [0, 1, 2, 3, 4, 5, 6]
        run(together(*[post_rows(b, blk, room, phase, ctx_tok[0]) for blk in range(4)]), 1000)
        run(together(*[post_logits(blk, room, phase) for blk in range(4)]), 1000)
        shared = post_shared(b, room, [*phase, *all_of(l_sx), DV.last(), AC.last()])
        routes = together(*[post_route(b, blk, room, phase) for blk in range(4)])
        for _ in routes:
            run(shared, 1)
        routed = [DV.last(), PL.last()]
        given = set()
        while len(given) < 4:
            given |= {k for k in free_banks if k < 4}
            free_banks[:] = [k for k in free_banks if k > 3]
            run(shared, 1)

        l_cs = line("l_cs")
        CS = view(ctxn[:, 0, 0:1], 0, [[128, 32], [1, 128]])
        hit = view(V[0][:, 0:1], 0, [[128, 32], [1, 128]])
        E0 = V[1][:, 0:1]
        idx2 = view(E0, 2304, [[1, NE]]).bitcast(i32)
        off, tf, ta = [view(E0, 2368 + 64 * i, [[1, NE]]) for i in range(3)]
        iof = view(E0, 2560, [[1, 128]])
        ioi = view(E0, 2688, [[1, 128]]).bitcast(i32)
        shift = view(E0, 2816, [[1, 128]])
        pick = view(E0, 2944, [[1, 2]])
        nsc, sc8 = view(E0, 2946, [[1, 1]]), view(E0, 2947, [[1, 1]])
        prev_c = view(E0, 2976, [[1, 32]])
        GC = view(E0, 3008, [[128, 4], [1, 128]])
        t2_ = view(E0, 3520, [[128, 4], [1, 128]])
        a = PL.op(lambda e: e.iota(ioi, pattern=[[1, 128]], base=0, channel_multiplier=0), *at_end)
        io_ready = PL.op(lambda e: e.tensor_copy(iof, ioi), a)
        a = PL.op(lambda e: e.memset(shift, 0.0))
        a = PL.op(lambda e: e.affine_select(out=shift, in_=shift, compare_op=ALU.not_equal, fill=1.0, base=1,
                                            pattern=[[-1, 128]], channel_multiplier=1), a)
        sh_ready = PL.op(lambda e: e.memset(shift[:, 64:65], 0.0), a)
        for h in range(2):
            a = DV.op(lambda e: e.tensor_scalar(pick[64 * h:64 * h + 64, 0:1], scol[64 * h:64 * h + 64, :], 128.0,
                                                -8064.0 - 8192.0 * h, ALU.mult, ALU.add), a)
        DV.op(lambda e: e.memset(pick[:, 1:2], 1.0))
        DV.op(lambda e: e.tensor_scalar(nsc, scol[:, 0:1], -1.0, None, ALU.mult))
        k_ready = DV.op(lambda e: e.tensor_scalar(sc8, scol[:, 0:1], 8064.0, None, ALU.add))
        for h in range(2):
            t = SP.dma(l_cs, CS[64 * h:64 * h + 64], CUM[32 * h:32 * h + 32].rearrange("e i t -> i e t"),
                       *all_of(l_cum), ctxn_free[0])
        p = PE.op(lambda e: e.matmul(ps[7][:, 0:32], shift, CS[:, :, 127], start=True, stop=True),
                  *take(7, sh_ready, t))
        prev_ready = DV.op(lambda e: e.tensor_copy(prev_c, ps[7][:, 0:32]), p)
        bank_free[7] = prev_ready

        order = [32 * (g % 2) + 8 * (g // 2) + i for g in range(8) for i in range(8)]
        idx_ready = {}
        g_state = {"hit": {}, "r": None}

        def find_hits(c):
            for i in range(2):
                sl = slice(8 * c + 4 * i, 8 * c + 4 * i + 4)
                s4 = view(iof, 0, [[0, 4], [1, 128]])
                last = view(CS[:, sl, 127:128], 0, [[128, 4], [0, 128]])
                a = DV.op(lambda e: e.tensor_tensor(hit[:, sl, :], s4, view(prev_c, 8 * c + 4 * i,
                                                                           [[1, 4], [0, 128]]), ALU.is_ge),
                          prev_ready, io_ready)
                m = DV.op(lambda e: e.tensor_tensor(t2_, s4, last, ALU.is_lt), t, g_state["r"])
                g_state["r"] = g_state["hit"][c, i] = DV.op(
                    lambda e: e.tensor_tensor(hit[:, sl, :], hit[:, sl, :], t2_, ALU.mult), a, m)

        def find_slots(g):
            h, c = g % 2, g // 2
            for i in range(2):
                while not free_banks:
                    next(shared)
                k = free_banks.pop(0)
                rows_ = slice(64 * h, 64 * h + 64)
                e0 = 32 * h + 8 * c + 4 * i
                for j in range(4):
                    e_ = 8 * c + 4 * i + j
                    p = PE.op(lambda e: e.matmul(ps[k][:, 128 * j:128 * j + 128], hit[rows_, e_, :], CS[rows_, e_, :],
                                                 start=True, stop=True), *take(k, g_state["hit"][c, i], t), inc=False)
                    p = PE.op(lambda e: e.matmul(ps[7][:, 2 * (e0 + j):2 * (e0 + j) + 2], hit[rows_, e_, :],
                                                 pick[rows_, :], start=True, stop=True), *take(7, k_ready),
                              inc=(j == 3))
                sl = slice(e0, e0 + 4)
                u = DV.op(lambda e: e.tensor_scalar(tf[:, sl], view(ps[7][:, 0:1], 2 * e0 + 1, [[2, 4]]),
                                                    nsc, sc8, ALU.mult, ALU.add), p, k_ready)
                u = DV.op(lambda e: e.tensor_tensor(ta[:, sl], view(ps[7][:, 0:1], 2 * e0, [[2, 4]]), tf[:, sl],
                                                    ALU.add), u)
                bank_free[7] = u
                gc = DV.op(lambda e: e.tensor_scalar(GC, view(ps[k][:, 0:1], 0, [[128, 4], [1, 128]]), scol[:, 0:1],
                                                     None, ALU.is_le), p, g_state.get("gc"))
                bank_free[k] = gc
                free_banks.append(k)
                r = DV.op(lambda e: e.tensor_reduce(off[:, sl], GC, AX.X, ALU.add), gc)
                g_state["gc"] = r
                r = DV.op(lambda e: e.tensor_tensor(tf[:, sl], off[:, sl], ta[:, sl], ALU.add), r, u)
                idx_ready[g] = DV.op(lambda e: e.tensor_copy(idx2[:, sl], tf[:, sl]), r)

        NX = 6
        l_ew = [line(f"l_ew{i}") for i in range(NX)]
        l_xe = [line(f"l_xe{i}") for i in range(NX)]
        l_sc = [line(f"l_sc{i}") for i in range(NCH)]
        W1 = TB[:, 0:1]
        WX = 8192
        wgu = [view(W1, WX + 768 * i, [[256, 2], [1, 256]]) for i in range(NX)]
        wdn = [view(W1, WX + 768 * i + 512, [[1, 256]]) for i in range(NX)]
        xe = [view(W1, WX + 4608 + 320 * i, [[1, 320]]) for i in range(NX)]
        ye = [view(E0, 256 * i, [[1, 256]]) for i in range(NX)]
        xeT = [view(E0, 1536 + 256 * i, [[128, 2], [1, 128]]) for i in range(2)]
        ae = [view(E0, 2048 + 128 * i, [[1, 128]]) for i in range(2)]
        w_free, x_free, xT_free, a_free, y_free = [None] * NX, [None] * NX, [None] * 2, [None] * 2, [None] * NX
        ew, xt = {}, {}
        begun = [*at_end, *routed, *all_of(l_w2), *all_of(l_cum)]
        GN = 8

        def load_expert(n):
            s = n % NX
            SP.dma(l_ew[s], wgu[s], egu_w[order[n]].rearrange("(k p) f -> p k f", p=128), w_free[s], *begun)
            ew[n] = SP.dma(l_ew[s], wdn[s], edn_w[order[n]], w_free[s])

        def gather_expert(n):
            s = n % NX
            xt[n] = PL.transfer(l_xe[s], lambda e: e.indirect_dma_start(
                xe[s], None, XH, bass.IndirectOffsetOnAxis(ap=idx2[:, order[n]:order[n] + 1].bitcast(u32), axis=0)),
                idx_ready[n // GN], x_free[s], *begun, *all_of(l_sh), zero_sent)

        l_px = line("l_px")
        x1s = [view(ZB[:, 0:1], 1024 * i, [[256, 4], [1, 256]]) for i in range(10)]
        for i in range(len(x1s)):
            SP.dma(l_px, x1s[i], X1v[i], *all_of(l_sx), *begun, AC.last())

        AHEAD = NX - 2
        for n in range(AHEAD):
            load_expert(n)
        find_hits(0)
        find_slots(0)
        for n in range(AHEAD):
            gather_expert(n)
        find_slots(1)
        sc_tok = [None] * NCH
        pend = {}

        def finish(n):
            s, c = n % NX, (n % NCH if n >= 14 else 1 + n % (NCH - 1))
            sc_tok[c] = PL.transfer(l_sc[c], lambda e: e.indirect_dma_start(
                Y[c], bass.IndirectOffsetOnAxis(ap=idx2[:, order[n]:order[n] + 1].bitcast(u32), axis=0), ye[s], None,
                compute_op=ALU.add), pend[n], sc_tok[c], *([l_y.done()] if c == 0 else [l_zy.done()]), zero_sent)
            y_free[s] = sc_tok[c]

        xT_tok, a_tok = {}, {}

        def turn_rows(n):
            s, s2, k = n % NX, n % 2, n % 2
            for c in range(2):
                p = PE.op(lambda e: e.transpose(ps[k][:, 128 * c:128 * c + 128], xe[s][:, 128 * c:128 * c + 128],
                                                ident[:, :]), *take(k, xt[n]), inc=(c == 1))
            xT_tok[n] = bank_free[k] = DV.op(lambda e: e.tensor_copy(
                xeT[s2], view(ps[k][:, 0:1], 0, [[128, 2], [1, 128]])), p, xT_free[s2], *begun)

        def gate_rows(n):
            s, s2, k = n % NX, n % 2, 2
            for f in range(2):
                for c in range(2):
                    p = PE.op(lambda e: e.matmul(
                        ps[k][:, 128 * f:128 * f + 128], wgu[s][:, c, 128 * f:128 * f + 128], xeT[s2][:, c, :],
                        start=(c == 0), stop=(c == 1)), *take(k, xT_tok[n], ew[n]), inc=(f == 1 and c == 1))
            xT_free[s2] = p
            a = AC.op(lambda e: e.activation(ae[s2], ps[k][:, 0:128], ACT.Silu), p, a_free[s2], *begun)
            a_tok[n] = bank_free[k] = DV.op(lambda e: e.tensor_tensor(ae[s2], ae[s2], ps[k][:, 128:256], ALU.mult),
                                            a)

        def down_rows(n):
            s, s2, k = n % NX, n % 2, 3
            p = PE.op(lambda e: e.matmul(ps[k][:, 0:256], ae[s2], wdn[s], start=True, stop=True),
                      *take(k, a_tok[n]))
            a_free[s2] = w_free[s] = p
            pend[n] = AC.op(lambda e: e.activation(ye[s], ps[k][:, 0:256], ACT.Copy,
                                                   scale=xe[s][:, C + order[n]:C + order[n] + 1]), p, y_free[s])
            bank_free[k] = x_free[s] = pend[n]

        for n in range(-1, NE + 1):
            if n % (2 * GN) == 2 and n // (2 * GN) + 1 < 4:
                find_hits(n // (2 * GN) + 1)
            if n % GN == 3 and n // GN + 2 < NE // GN:
                find_slots(n // GN + 2)
            if 0 <= n and n + AHEAD < NE:
                load_expert(n + AHEAD)
                gather_expert(n + AHEAD)
            run(shared, SHN)
            if n + 1 < NE:
                turn_rows(n + 1)
            if 0 <= n < NE:
                gate_rows(n)
            if n > 0:
                down_rows(n - 1)
            if n > 1:
                finish(n - 2)
        finish(NE - 1)
        run(shared, 100000)

        NF = 5
        l_f = [line(f"l_f{i}") for i in range(NF)]
        l_o = [line(f"l_o{i}") for i in range(NF)]
        F0 = TB[:, 0:1]
        yt = [[view(a_, o + 1024 * c, [[256, 4], [1, 256]]) for c in range(NCH + 1)]
              for a_, o in [(F0, 4096 * i) for i in range(4)] + [(scr[:, 0:1], 0)]]
        endt = [PE.last(), DV.last(), AC.last(), *all_of(l_sh), *all_of(l_w2)]
        NG = NTILE // 4
        f_tok, f_rs, f_in = {}, {}, {}
        nm = [view(V[1][:, 0:1], 4 * i, [[1, 4]]) for i in range(NF)]

        l_x1_done = l_px.done()

        def f_load(n):
            s = n % NF
            for c in range(NCH):
                SP.dma(l_f[s], yt[s][c], Yv[c][n], *sc_tok, l_y.done(), l_zy.done(), l_o[s].done(), *endt)
            f_in[n] = l_f[s].done()
            if n >= len(x1s):
                f_in[n] = SP.dma(l_f[s], yt[s][NCH], X1v[n], *all_of(l_sx))

        def f_sum(n):
            s = n % NF
            y = yt[s]
            v = f_in[n]
            if NCH > 2:
                v = PL.op(lambda e: e.tensor_tensor(y[1], y[1], y[2], ALU.add), v)
            v = DV.op(lambda e: e.tensor_tensor(y[0], y[0], y[1], ALU.add), v)
            r = rstd(s, lambda i: y[0][:, i, :], v)
            m = PL.op(lambda e: e.tensor_scalar(nm[s], view(mv[s][:, 0, 0:1], 0, [[2, 4]]), -1.0, None, ALU.mult),
                      r, *endt, f_tok.get(n - NF))
            for i in range(4):
                a = AC.op(lambda e: e.activation(y[0][:, i, :], y[0][:, i, :], ACT.Identity, bias=nm[s][:, i:i + 1],
                                                 scale=1.0), m, inc=(i == 3))
            f_tok[n] = a

        def f_out(n):
            s = n % NF
            y = yt[s]
            x = x1s[n] if n < len(x1s) else y[NCH]
            for i in range(4):
                v = DV.op(lambda e: e.scalar_tensor_tensor(y[0][:, i, :], y[0][:, i, :], rs[s][:, i:i + 1],
                                                           x[:, i, :], ALU.mult, ALU.add),
                          f_tok[n], l_x1_done, inc=(i == 3))
            ln_free[s] = v
            SP.dma(l_o[s], outv[n], y[0], v)

        for n in range(NF):
            f_load(n)
        f_sum(0)
        for n in range(NG):
            if n + 1 < NG:
                f_sum(n + 1)
            f_out(n)
            if n + NF < NG:
                f_load(n + NF)
        SP.wait(*all_of(l_o), *all_of(l_sc), l_y.done(), l_zy.done(), l_zero.done(), l_cs.done(), *all_of(l_cum),
                *all_of(l_w2), *all_of(l_sh), *all_of(l_sx), l_zq.done())


_A = 'L0_attn_'
_F = 'L0_ffn_'


def kernel(**inputs):
    import numpy as _np
    import concourse.bacc as _bacc
    from concourse import mybir as _mybir
    from concourse.bass_utils import run_bass_kernel_spmd as _run

    g = lambda n: _np.asarray(inputs[n])
    lay = {
        "x": g(_A + 'hidden_states'),
        "WqT": g(_A + 'Wq').T, "bq": g(_A + 'bq').reshape(2, 128).T,
        "WkT": g(_A + 'Wk').T, "bk": g(_A + 'bk').reshape(2, 128).T,
        "WvT": g(_A + 'Wv').T, "bv": g(_A + 'bv'),
        "WpT": g(_A + 'Wproj').reshape(16, 16, 16).transpose(2, 1, 0),
        "lbw": g(_A + 'log_bandwidth'),
        "gates_w": _np.concatenate([g(_F + 'gate_w'), g(_F + 'shared_gate_w')], axis=1),
        "sgu_w": g(_F + 'shared_gate_up_w'), "sdn_w": g(_F + 'shared_down_w'),
        "egu_w": g(_F + 'expert_gate_up_w'), "edn_w": g(_F + 'expert_down_w'),
    }
    nc = _bacc.Bacc("TRN2", target_bir_lowering=False, num_devices=1)
    arrays, args = {}, []
    for n, a in lay.items():
        a = _np.ascontiguousarray(a)
        arrays["in_" + n] = a
        args.append(nc.dram_tensor("in_" + n, a.shape, _mybir.dt.from_np(a.dtype), kind="ExternalInput").ap())
    out = nc.dram_tensor("out_0", (4, 2048, 256), _mybir.dt.float32, kind="ExternalOutput").ap()
    build(nc, *args, out)
    r = _run(nc, [arrays], core_ids=[0])
    return r.results[0]["out_0"]
```
